# Optimizing a Trainium2 kernel written in Bass

```python
import numpy as np
import jax
import jax.numpy as jnp

def _softmax(x, axis=-1):
    return jax.nn.softmax(x, axis=axis)

def _gelu(x):
    return jax.nn.gelu(x, approximate=True)

def _silu(x):
    return jax.nn.silu(x)

def _sigmoid(x):
    return jax.nn.sigmoid(x)

def _layernorm(x, axis=-1, eps=1e-05):
    m = jnp.mean(x, axis=axis, keepdims=True)
    v = jnp.var(x, axis=axis, keepdims=True)
    return (x - m) / jnp.sqrt(v + eps)

def _scatter_add(tgt, idx, src, axis=0):
    return tgt.at[idx].add(src)

def _segment_sum(src, seg, n):
    return jax.ops.segment_sum(src, seg, n)
kernel_name = 'mk_decoder_preln_d1_seqx_r4_4dd7c7'

def setup_inputs(seed: int=0):
    np.random.seed(seed)
    _w = jnp.asarray

    def _rec_inputs():
        import jax
        import jax.numpy as jnp
        _rk = jax.random.key(seed)
        x = 7.22e-05 + 1 * jax.random.normal(jax.random.fold_in(_rk, 1), (16, 512, 256), jnp.float32)
        _lenS = 512 - jax.random.randint(jax.random.fold_in(_rk, 7), (16,), 0, max(1, 512 // 4) + 1, jnp.int32)
        _lenS2 = 64 - jax.random.randint(jax.random.fold_in(_rk, 8), (16,), 0, max(1, 64 // 4) + 1, jnp.int32)
        _ctx_768P = jax.random.normal(jax.random.fold_in(_rk, 11), (16, 16, 192), jnp.float32)
        _ctx_768c = jax.random.dirichlet(jax.random.fold_in(_rk, 511), 0.3 * jnp.ones((16,), jnp.float32), (16, 64))
        _ctx_768t = jnp.einsum('bsk,bkd->bsd', _ctx_768c, _ctx_768P)
        _ctx_768t = _ctx_768t * jax.lax.rsqrt(jnp.mean(jnp.square(_ctx_768t)) + 1e-12) * 0.953939
        ctx_768 = -0.000191848 + 0.999787 * (_ctx_768t + 0.3 * jax.random.normal(jax.random.fold_in(_rk, 611), (16, 64, 192), jnp.float32))
        return (x, ctx_768)
    x, ctx_768 = _rec_inputs()

    def _L0_attn_setup():
        import jax, jax.numpy as jnp
        import numpy as np
        import math
        H = 16
        LORA_SCALING = 16 / 8
        NEG_INF = -1e+30

        def _alibi_slopes(n_heads):
            start = 2.0 ** (-2.0 ** (-(math.log2(n_heads) - 3)))
            return jnp.asarray([start * start ** i for i in range(n_heads)], dtype=jnp.float32)

        def _lora(x, W, A, Bm):
            return x @ W.T + x @ Bm.T @ A.T * LORA_SCALING
        key = jax.random.key(seed)
        ks = jax.random.split(key, 11)
        B, T, E, r = (4, 512, 256, 8)
        d = {'x': jax.random.normal(ks[0], (B, T, E), jnp.float32), 'Wq': jax.random.normal(ks[1], (E, E), jnp.float32) * E ** (-0.5), 'Aq': jax.random.normal(ks[2], (E, r), jnp.float32) * 0.01, 'Bq': jax.random.normal(ks[3], (r, E), jnp.float32) * 0.01, 'Wk': jax.random.normal(ks[4], (E, E), jnp.float32) * E ** (-0.5), 'Ak': jax.random.normal(ks[5], (E, r), jnp.float32) * 0.01, 'Bk': jax.random.normal(ks[6], (r, E), jnp.float32) * 0.01, 'Wv': jax.random.normal(ks[7], (E, E), jnp.float32) * E ** (-0.5), 'Av': jax.random.normal(ks[8], (E, r), jnp.float32) * 0.01, 'Bv': jax.random.normal(ks[9], (r, E), jnp.float32) * 0.01, 'Wp': jax.random.normal(ks[10], (E, E), jnp.float32) * E ** (-0.5)}
        return d
    _L0_attn_all = _L0_attn_setup()
    _L0_attn_in = {k: v for k, v in _L0_attn_all.items() if k in ('Wq', 'Aq', 'Bq', 'Wk', 'Ak', 'Bk', 'Wv', 'Av', 'Bv', 'Wp')}
    del _L0_attn_all

    def _L0_xattn_setup():
        import jax, jax.numpy as jnp
        import numpy as np
        N_HEADS = 16
        key = jax.random.key(seed)
        ks = jax.random.split(key, 8)
        b, l, m = (8, 256, 256)
        d_embed, d_cross = (256, 192)
        s_q = 1.0 / np.sqrt(d_embed)
        s_kv = 1.0 / np.sqrt(d_cross)
        return {'x': jax.random.normal(ks[0], (b, l, d_embed), jnp.float32), 'y': jax.random.normal(ks[1], (b, m, d_cross), jnp.float32), 'Wq': jax.random.normal(ks[2], (d_embed, d_embed), jnp.float32) * s_q, 'bq': jax.random.normal(ks[3], (d_embed,), jnp.float32) * 0.01, 'Wkv': jax.random.normal(ks[4], (2 * d_embed, d_cross), jnp.float32) * s_kv, 'bkv': jax.random.normal(ks[5], (2 * d_embed,), jnp.float32) * 0.01, 'Wo': jax.random.normal(ks[6], (d_embed, d_embed), jnp.float32) * s_q, 'bo': jax.random.normal(ks[7], (d_embed,), jnp.float32) * 0.01}
    _L0_xattn_all = _L0_xattn_setup()
    _L0_xattn_in = {k: v for k, v in _L0_xattn_all.items() if k in ('Wq', 'bq', 'Wkv', 'bkv', 'Wo', 'bo')}
    del _L0_xattn_all

    def _L0_ffn_setup():
        import jax, jax.numpy as jnp
        import numpy as np
        NUM_EXPERTS = 8
        TOP_K = 2

        def _swiglu(x, w1, w2, w3):
            return jax.nn.silu(x @ w1) * (x @ w3) @ w2
        key = jax.random.key(seed)
        ks = jax.random.split(key, 9)
        B, S, D, H, E = (1, 256, 256, 256, NUM_EXPERTS)
        std = 0.02
        return {'x': jax.random.normal(ks[0], (B, S, D), jnp.float32), 'router_w': jax.random.normal(ks[1], (D, E), jnp.float32) * std, 'expert_bias': jnp.zeros((E,), jnp.float32), 'w1': jax.random.normal(ks[2], (E, D, H), jnp.float32) * std, 'w2': jax.random.normal(ks[3], (E, H, D), jnp.float32) * std, 'w3': jax.random.normal(ks[4], (E, D, H), jnp.float32) * std, 'sw1': jax.random.normal(ks[5], (D, H), jnp.float32) * std, 'sw2': jax.random.normal(ks[6], (H, D), jnp.float32) * std, 'sw3': jax.random.normal(ks[7], (D, H), jnp.float32) * std}
    _L0_ffn_all = _L0_ffn_setup()
    _L0_ffn_in = {k: v for k, v in _L0_ffn_all.items() if k in ('router_w', 'expert_bias', 'w1', 'w2', 'w3', 'sw1', 'sw2', 'sw3')}
    del _L0_ffn_all
    return {'x': x, 'ctx_768': ctx_768, 'L0_attn_Wq': _L0_attn_in['Wq'], 'L0_attn_Aq': _L0_attn_in['Aq'], 'L0_attn_Bq': _L0_attn_in['Bq'], 'L0_attn_Wk': _L0_attn_in['Wk'], 'L0_attn_Ak': _L0_attn_in['Ak'], 'L0_attn_Bk': _L0_attn_in['Bk'], 'L0_attn_Wv': _L0_attn_in['Wv'], 'L0_attn_Av': _L0_attn_in['Av'], 'L0_attn_Bv': _L0_attn_in['Bv'], 'L0_attn_Wp': _L0_attn_in['Wp'], 'L0_xattn_Wq': _L0_xattn_in['Wq'], 'L0_xattn_bq': _L0_xattn_in['bq'], 'L0_xattn_Wkv': _L0_xattn_in['Wkv'], 'L0_xattn_bkv': _L0_xattn_in['bkv'], 'L0_xattn_Wo': _L0_xattn_in['Wo'], 'L0_xattn_bo': _L0_xattn_in['bo'], 'L0_ffn_router_w': _L0_ffn_in['router_w'], 'L0_ffn_expert_bias': _L0_ffn_in['expert_bias'], 'L0_ffn_w1': _L0_ffn_in['w1'], 'L0_ffn_w2': _L0_ffn_in['w2'], 'L0_ffn_w3': _L0_ffn_in['w3'], 'L0_ffn_sw1': _L0_ffn_in['sw1'], 'L0_ffn_sw2': _L0_ffn_in['sw2'], 'L0_ffn_sw3': _L0_ffn_in['sw3']}

def reference(x, ctx_768, L0_attn_Wq, L0_attn_Aq, L0_attn_Bq, L0_attn_Wk, L0_attn_Ak, L0_attn_Bk, L0_attn_Wv, L0_attn_Av, L0_attn_Bv, L0_attn_Wp, L0_xattn_Wq, L0_xattn_bq, L0_xattn_Wkv, L0_xattn_bkv, L0_xattn_Wo, L0_xattn_bo, L0_ffn_router_w, L0_ffn_expert_bias, L0_ffn_w1, L0_ffn_w2, L0_ffn_w3, L0_ffn_sw1, L0_ffn_sw2, L0_ffn_sw3):
    import jax
    import jax.numpy as jnp

    def _L0_attn_ref(x, Wq, Aq, Bq, Wk, Ak, Bk, Wv, Av, Bv, Wp):
        import jax, jax.numpy as jnp
        import numpy as np
        import math
        H = 16
        LORA_SCALING = 16 / 8
        NEG_INF = -1e+30

        def _alibi_slopes(n_heads):
            start = 2.0 ** (-2.0 ** (-(math.log2(n_heads) - 3)))
            return jnp.asarray([start * start ** i for i in range(n_heads)], dtype=jnp.float32)

        def _lora(x, W, A, Bm):
            return x @ W.T + x @ Bm.T @ A.T * LORA_SCALING
        B, T, E = x.shape
        dh = E // H
        q = _lora(x, Wq, Aq, Bq).reshape(B, T, H, dh).transpose(0, 2, 1, 3)
        k = _lora(x, Wk, Ak, Bk).reshape(B, T, H, dh).transpose(0, 2, 1, 3)
        v = _lora(x, Wv, Av, Bv).reshape(B, T, H, dh).transpose(0, 2, 1, 3)
        s = jnp.einsum('bhqd,bhkd->bhqk', q, k) / jnp.sqrt(jnp.float32(dh))
        i = jnp.arange(T)[:, None]
        j = jnp.arange(T)[None, :]
        slopes = _alibi_slopes(H)
        bias = slopes[:, None, None] * (i - j).astype(jnp.float32)
        s = s + bias[None]
        s = jnp.where(j[None, None] <= i[None, None], s, NEG_INF)
        out = jnp.einsum('bhqk,bhkd->bhqd', jax.nn.softmax(s, axis=-1), v)
        out = out.transpose(0, 2, 1, 3).reshape(B, T, E)
        return out @ Wp.T

    def _L0_xattn_ref(x, y, Wq, bq, Wkv, bkv, Wo, bo):
        import jax, jax.numpy as jnp
        import numpy as np
        N_HEADS = 16
        b, l, d = x.shape
        m = y.shape[1]
        h = N_HEADS
        dh = d // h
        q = (jnp.einsum('bld,ed->ble', x, Wq) + bq).reshape(b, l, h, dh)
        kv = (jnp.einsum('bmc,ec->bme', y, Wkv) + bkv).reshape(b, m, h, 2 * dh)
        k, v = (kv[..., :dh], kv[..., dh:])
        scale = 1.0 / jnp.sqrt(jnp.asarray(dh, x.dtype))
        att = jax.nn.softmax(jnp.einsum('blhd,bmhd->blmh', q, k) * scale, axis=2)
        out = jnp.einsum('blmh,bmhd->blhd', att, v).reshape(b, l, d)
        return jnp.einsum('bld,ed->ble', out, Wo) + bo

    def _L0_ffn_ref(x, router_w, expert_bias, w1, w2, w3, sw1, sw2, sw3):
        import jax, jax.numpy as jnp
        import numpy as np
        NUM_EXPERTS = 8
        TOP_K = 2

        def _swiglu(x, w1, w2, w3):
            return jax.nn.silu(x @ w1) * (x @ w3) @ w2
        B, S, D = x.shape
        E, K = (NUM_EXPERTS, TOP_K)
        N = B * S
        x_flat = x.reshape(N, D)
        logits = x_flat @ router_w
        scores = jax.nn.softmax(logits.astype(jnp.float32), axis=-1)
        _, sel = jax.lax.top_k(scores + expert_bias[None, :], K)
        top_scores = jnp.take_along_axis(scores, sel, axis=-1)
        flat_exp = sel.reshape(-1)
        order = jnp.argsort(flat_exp)
        exp_sorted = flat_exp[order]
        routed_input = x_flat[order // K]
        routed_output = jnp.zeros_like(routed_input)
        for e in range(E):
            mask = (exp_sorted == e)[:, None]
            y_e = _swiglu(routed_input, w1[e], w2[e], w3[e])
            routed_output = routed_output + jnp.where(mask, y_e, 0.0)
        unsorted = jnp.zeros((N * K, D), routed_output.dtype).at[order].set(routed_output)
        unsorted = unsorted.reshape(N, K, D)
        out_experts = jnp.einsum('nk,nkd->nd', top_scores, unsorted)
        shared_out = _swiglu(x_flat, sw1, sw2, sw3)
        return (shared_out + out_experts).reshape(B, S, D)
    x = x + _L0_attn_ref(_layernorm(x, axis=-1), L0_attn_Wq, L0_attn_Aq, L0_attn_Bq, L0_attn_Wk, L0_attn_Ak, L0_attn_Bk, L0_attn_Wv, L0_attn_Av, L0_attn_Bv, L0_attn_Wp)
    x = x + _L0_xattn_ref(_layernorm(x, axis=-1), ctx_768, L0_xattn_Wq, L0_xattn_bq, L0_xattn_Wkv, L0_xattn_bkv, L0_xattn_Wo, L0_xattn_bo)
    x = x + _L0_ffn_ref(_layernorm(x, axis=-1), L0_ffn_router_w, L0_ffn_expert_bias, L0_ffn_w1, L0_ffn_w2, L0_ffn_w3, L0_ffn_sw1, L0_ffn_sw2, L0_ffn_sw3)
    return x

_drawn_inputs = setup_inputs


def setup_inputs(seed=0):
    import zlib

    import numpy as np

    out = dict(_drawn_inputs(seed))
    spreads = {'L0_ffn_expert_bias': (0.0, 0.8)}
    factors = {'L0_attn_Aq': 8.0,
     'L0_attn_Bq': 8.0,
     'L0_attn_Ak': 8.0,
     'L0_attn_Bk': 8.0,
     'L0_attn_Av': 8.0,
     'L0_attn_Bv': 8.0,
     'L0_xattn_bq': 8.0,
     'L0_xattn_bkv': 7.242,
     'L0_xattn_bo': 6.683,
     'L0_ffn_router_w': 8.0,
     'L0_ffn_w1': 8.0,
     'L0_ffn_w2': 8.0,
     'L0_ffn_w3': 8.0,
     'L0_ffn_sw1': 4.063,
     'L0_ffn_sw2': 4.019,
     'L0_ffn_sw3': 4.019}
    for name, (base, spread) in spreads.items():
        noise = np.random.default_rng([zlib.crc32(name.encode()), seed]).standard_normal(out[name].shape)
        drawn = base * np.exp(spread * noise) if base else spread * noise
        out[name] = jnp.asarray(drawn.astype(out[name].dtype))
    for name, factor in factors.items():
        out[name] = (out[name] * factor).astype(out[name].dtype)
    return out
```

```python
from contextlib import ExitStack

import numpy as np

import concourse.bass as bass
from concourse import mybir

F32 = mybir.dt.float32
F32R = mybir.dt.float32r
BF16 = mybir.dt.bfloat16
U32 = mybir.dt.uint32
ALU = mybir.AluOpType
ACT = mybir.ActivationFunctionType
AX = mybir.AxisListType

P = 128
B, T, D = 16, 512, 256
H, DH = 16, 16
M, DC = 64, 192
R = 8
E, HID = 8, 256
NE = E + 1
EPS = 1e-5
NQ = T // P
NC = D // P
HC = H // NC
GH = 4
VW = 32
NG = H // GH
NP_TILES = 7
ONES_ROW, BIAS_ROW, MAX_ROW = 64, 64, 96
MASKED = -1.0e30
LOWEST = -3.0e38

PARTS = [[(0, 0, 512)], [(1, 0, 384), (3, 384, 128)], [(2, 0, 256)]]

PASS1_AT = {0: (8, 9), 1: (10, 11), 2: (12,), 3: (13,), 4: (14, 15)}
M1_STEP = 5
DVE_STEPS = (1, NG, 1 + NG)


class Signal:

    def __init__(self, sem, project=0, attend=0, cross=0, first=0):
        self.sem, self.first = sem, first
        self.per = {"project": project, "attend": attend, "cross": cross}


class Section:

    def __init__(self, name, i=None, last=False):
        self.name, self.i, self.last = name, i, last

    def __call__(self, signal, n):
        per = signal.per
        value = signal.first + n
        if self.i is None:
            return value
        value += per["project"]
        if self.name in ("attend", "cross") and not self.last:
            value += per["project"]
        if self.name == "cross":
            value += per["attend"]
        return self.i * sum(per.values()) + value


def attention(nc, a, x2_dram):
    ctx = ExitStack()
    with ctx:
        def sb(name, shape, dt=F32):
            return ctx.enter_context(nc.sbuf_tensor(name, shape, dt))

        def bank(name):
            return ctx.enter_context(nc.psum_tensor(name, [P, 512], F32))

        def sem(name):
            return ctx.enter_context(nc.semaphore(name))

        eye = sb("eye", [P, P])
        eye_bf = sb("eye_bf", [P, P], BF16)
        tri_bf = sb("tri_bf", [P, P], BF16)
        row_mask = sb("row_mask", [P, T])
        head_mask = sb("head_mask", [P, HC, M])
        pick_max = sb("pick_max", [2 * 32, H // 2, P], F32R)
        power = sb("power", [P, NQ])
        names = ("q", "k", "v", "p", "xq", "xk", "xv", "xo")
        w_hi = {n: sb(f"w_{n}_hi", [P, NC, D], F32R) for n in names}
        w_lo = {n: sb(f"w_{n}_lo", [P, NC, D], F32R) for n in names}
        xq_bias = sb("xq_bias", [P, NC])
        xk_bias = sb("xk_bias", [P, NC])
        xv_bias = sb("xv_bias", [P, D])
        xo_bias = sb("xo_bias", [P, D])

        q_stack = sb("q_stack", [P, H, T], F32R)
        k_stack = sb("k_stack", [P, H, T], F32R)
        x_in = sb("x_in", [P, NQ, D])
        x_norm = sb("x_norm", [P, NQ, D])
        x_res = sb("x_res", [P, NQ, D])
        x_out = sb("x_out", [P, NQ, D])
        stats = sb("stats", [P, NQ, 6])
        mean_var = sb("mean_var", [P, NQ, 2])
        rstd = sb("rstd", [P, NQ])
        feat_hi = sb("feat_hi", [P, NC, T], F32R)
        feat_lo = sb("feat_lo", [P, NC, T], F32R)
        qk = [sb(f"qk{n}", [P, NC, T], F32R) for n in range(4)]
        v_next = sb("v_next", [P, NQ, D])
        v_ones = sb("v_ones", [P, NQ, H, VW])
        scratch = sb("scratch", [P, 2, T])
        row_max = sb("row_max", [P, NQ, H])
        max_hi = sb("max_hi", [HC, T], F32R)
        max_lo = sb("max_lo", [HC, T], F32R)
        xmax = sb("xmax", [2 * 32, T], F32R)
        probs = [sb(f"probs{n}", [P, T]) for n in range(NP_TILES)]
        o_ext = [sb(f"o_ext{n}", [P, T]) for n in range(2)]
        o_sum = sb("o_sum", [P, 2, NQ, GH])
        o_tok = sb("o_tok", [P, NQ, D])
        ctx_in = sb("ctx_in", [P, 2, M])
        ctx_hi = sb("ctx_hi", [P, 2, 2 * M], F32R)
        ctx_lo = sb("ctx_lo", [P, 2, 2 * M], F32R)
        xk_hi = sb("xk_hi", [P, NC, M], F32R)
        xk_lo = sb("xk_lo", [P, NC, M], F32R)
        xk_hi_heads = sb("xk_hi_heads", [P, NC, HC * M], F32R)
        xk_lo_heads = sb("xk_lo_heads", [P, NC, HC * M], F32R)
        xv_ones = sb("xv_ones", [P, H // 2, 2 * VW])

        scores = [bank(f"scores{n}") for n in range(2)]
        scores_t = [bank(f"scores_t{n}") for n in range(2)]
        outs = [bank(f"outs{n}") for n in range(2)]
        work = [bank(f"work{n}") for n in range(2)]

        stack_dram = nc.dram_tensor("stack_dram", (4, NC, HC, DH, T), F32, kind="Internal").ap()

        w_loaded = sem("w_loaded")
        c_loaded = sem("c_loaded")
        lora_ready = sem("lora_ready")
        zeroed = sem("zeroed")
        pool_step = sem("pool_step")
        prep_step = sem("prep_step")
        alibi_loaded = [sem(f"alibi_loaded{n}") for n in range(2)]
        alibi_used = sem("alibi_used")
        raw = {n: (x_in, x_norm, x_res, x_out)[j // 2][:, 2 * (j % 2):2 * (j % 2) + 2, :]
               for j, n in enumerate(names)}
        with ExitStack() as prep:
            def tmp(name, shape, dt=F32):
                return prep.enter_context(nc.sbuf_tensor(name, shape, dt))

            lora_a = {n: probs[j][0:R, 0:D] for j, n in enumerate(("q", "k", "v"))}
            lora_b = {n: probs[j][0:R, D:2 * D] for j, n in enumerate(("q", "k", "v"))}
            alibi = (v_next, o_tok)
            block = prep.enter_context(nc.Block())

            @block.sync
            def _(sp):
                for n in names:
                    src = a["w_" + n]
                    if src.shape[0] == D:
                        sp.dma_start(raw[n], src.rearrange("(c p) n -> p c n", p=P)).then_inc(w_loaded, 16)
                sp.wait_ge(zeroed, 1)
                for n in ("xk", "xv"):
                    sp.dma_start(raw[n][:, 0, :], a["w_" + n][0:P, :]).then_inc(w_loaded, 16)
                    sp.dma_start(raw[n][0:DC - P, 1, :], a["w_" + n][P:DC, :]).then_inc(w_loaded, 16)
                for n in ("q", "k", "v"):
                    sp.dma_start(lora_a[n], a["a_" + n]).then_inc(w_loaded, 16)
                    sp.dma_start(lora_b[n], a["b_" + n]).then_inc(w_loaded, 16)
                for dst, src in ((eye, "eye"), (row_mask, "row_mask"), (xv_bias, "xv_bias"),
                                 (xo_bias, "xo_bias"), (xq_bias, "xq_bias"), (xk_bias, "xk_bias")):
                    sp.dma_start(dst[:], a[src]).then_inc(c_loaded, 16)
                sp.dma_start(head_mask[:], a["head_mask"]).then_inc(c_loaded, 16)
                sp.dma_start(scratch[:, 0, 0:P], a["tri"]).then_inc(c_loaded, 16)
                sp.dma_start(o_tok[0:2 * 32, :, :], a["pick_max"]).then_inc(c_loaded, 16)
                for part in range(H // 2):
                    sp.wait_ge(alibi_used, max(part - 1, 0) + 2)
                    sp.dma_start(alibi[part % 2][BIAS_ROW:BIAS_ROW + 2, :, :], a["alibi"][:, part])\
                      .then_inc(alibi_loaded[part % 2], 16)

            @block.tensor
            def _(pe):
                pe.wait_ge(w_loaded, 16 * 16)
                for j, n in enumerate(("q", "k", "v")):
                    for c in range(NC):
                        pe.matmul((scores + scores_t + outs)[2 * j + c][:, 0:D],
                                  lora_b[n][:, c * P:(c + 1) * P], lora_a[n][:, :],
                                  start=True, stop=True).then_inc(lora_ready, 1)

            @block.gpsimd
            def _(pool):
                pool.memset(raw["xk"][:, 1, :], 0.0)
                pool.memset(raw["xv"][:, 1, :], 0.0).then_inc(zeroed, 1)
                pool.memset(ctx_in[:], 0.0)
                pool.memset(power[:], -0.5)
                pool.memset(v_ones[:], 0.0).then_inc(pool_step, 1)
                pool.memset(xv_ones[:], 0.0).then_inc(pool_step, 1)
                pool.wait_ge(pool_step, 2)
                pool.memset(v_ones[:, :, :, DH:DH + 1], 1.0).then_inc(pool_step, 1)
                pool.wait_ge(pool_step, 3)
                pool.memset(xv_ones[0:M, :, DH:DH + 1], 1.0).then_inc(pool_step, 1)
                pool.wait_ge(pool_step, 4)
                pool.memset(xv_ones[M:P, :, VW + DH:VW + DH + 1], 1.0).then_inc(pool_step, 1)

            @block.vector
            def _(dve):
                count = [0]

                def link(ins):
                    count[0] += 1
                    ins.then_inc(prep_step, 1)
                    dve.wait_ge(prep_step, count[0])

                link(dve.memset(q_stack[:].bitcast(F32), 0.0))
                link(dve.memset(k_stack[:].bitcast(F32), 0.0))
                dve.memset(xmax[:].bitcast(F32), 0.0)
                dve.memset(q_stack[ONES_ROW:ONES_ROW + 2, :, :].bitcast(F32), 1.0)
                dve.memset(k_stack[MAX_ROW:MAX_ROW + 2, :, :].bitcast(F32), 1.0)
                dve.wait_ge(w_loaded, 16 * 16)
                dve.wait_ge(c_loaded, 16 * 9)
                dve.tensor_copy(eye_bf[:], eye[:])
                dve.tensor_copy(tri_bf[:], scratch[:, 0, 0:P])
                dve.tensor_copy(pick_max[:].rearrange("p a b -> p (a b)"),
                                o_tok[0:2 * 32, :, :].rearrange("p a b -> p (a b)"))\
                    .then_inc(alibi_used, 2)
                dve.wait_ge(lora_ready, 2 * 3)
                for j, n in enumerate(("q", "k", "v")):
                    for c in range(NC):
                        link(dve.scalar_tensor_tensor(
                            out=raw[n][:, c, :], in0=(scores + scores_t + outs)[2 * j + c][:, 0:D],
                            scalar=2.0, in1=raw[n][:, c, :], op0=ALU.mult, op1=ALU.add))
                link(dve.tensor_scalar(raw["q"], raw["q"], DH ** -0.5, None, ALU.mult))
                link(dve.tensor_scalar(raw["xq"], raw["xq"], DH ** -0.5, None, ALU.mult))
                dve.tensor_scalar(xq_bias[:], xq_bias[:], DH ** -0.5, None, ALU.mult)
                for n in names:
                    link(dve.tensor_copy(w_hi[n][:], raw[n]))
                    dve.tensor_tensor(w_lo[n][:], raw[n], w_hi[n][:].bitcast(F32), ALU.subtract)
                for part in range(H // 2):
                    dve.wait_ge(alibi_loaded[part % 2], 16 * (part // 2 + 1))
                    dve.tensor_copy(
                        k_stack[BIAS_ROW:BIAS_ROW + 2, 2 * part:2 * part + 2, :],
                        alibi[part % 2][BIAS_ROW:BIAS_ROW + 2, :, :].rearrange("r (h u) d -> r h (u d)", h=2))\
                        .then_inc(alibi_used, 1)

        pause, pool_pause = sem("pause"), sem("pool_pause")
        work_ready = Signal(sem("work_ready"), 8, 13, 13)
        work_hi = Signal(sem("work_hi"), 6, 6, 7)
        work_free = Signal(sem("work_free"), 8, 13, 13, first=2)
        scores_ready = Signal(sem("scores_ready"), 0, NQ * H, 2 * NQ)
        scores_read = Signal(sem("scores_read"), 0, NQ * H, 2 * NQ, first=2)
        scores_t_ready = Signal(sem("scores_t_ready"), 0, 3 * H, H // 2)
        exp_done = Signal(sem("exp_done"), 0, 3 * H, H // 2, first=2)
        probs_used = Signal(sem("probs_used"), 0, 3 * H, H // 2, first=NP_TILES)
        outs_read = Signal(sem("outs_read"), 0, NG, NG, first=2)
        x_in_loaded = Signal(sem("x_in_loaded"), 16)
        var_ready = Signal(sem("var_ready"), 1, 0, 1)
        rstd_ready = Signal(sem("rstd_ready"), 1, 0, 1)
        norm_ready = Signal(sem("norm_ready"), 1, 0, 1)
        qk_stored = Signal(sem("qk_stored"), 4 * 16)
        stack_loaded = [Signal(sem(f"stack_loaded{u}"), 6 * 16) for u in range(2)]
        max_loaded = [Signal(sem(f"max_loaded{u}"), 0, 2 * 16) for u in range(2)]
        v_ready = Signal(sem("v_ready"), 1)
        x_res_loaded = Signal(sem("x_res_loaded"), 16)
        ctx_loaded = Signal(sem("ctx_loaded"), 2 * 16)
        ctx_split = Signal(sem("ctx_split"), 0, 1)
        ctx_step = Signal(sem("ctx_step"), 0, 1)
        heads_ready = Signal(sem("heads_ready"), 0, 1)
        bias_added = Signal(sem("bias_added"), 0, 0, 1)
        eps_added = Signal(sem("eps_added"), 1, 0, 1)
        dve_step = Signal(sem("dve_step"), *DVE_STEPS)
        x2_stored = Signal(sem("x2_stored"), 0, 0, 2 * 16, first=1)

        xb = a["x"].rearrange("b (q p) d -> b p q d", p=P)
        x2b = x2_dram.rearrange("b (q p) d -> b p q d", p=P)

        def work_bank(sec, n):
            return work[(n + (13 if sec.name == "cross" else 0)) % 2]

        block = ctx.enter_context(nc.Block())

        @block.sync
        def _(sp):
            sp.sem_inc(x2_stored.sem, 1)

            def load_x_in(b):
                sp.dma_start(x_in[:], xb[b]).then_inc(x_in_loaded.sem, 16)

            def load_x_res(b):
                sp.dma_start(x_res[:], xb[b]).then_inc(x_res_loaded.sem, 16)

            def load_ctx(b):
                sp.dma_start(ctx_in[:, 0, :], a["ctx"][b, 0:P, :]).then_inc(ctx_loaded.sem, 16)
                sp.dma_start(ctx_in[0:DC - P, 1, :], a["ctx"][b, P:DC, :]).then_inc(ctx_loaded.sem, 16)

            def store_qk(sec):
                for n in range(4):
                    if n % 2 == 0:
                        sp.wait_ge(work_free.sem, sec(work_free, 4 + n))
                    sp.dma_start(stack_dram[n].rearrange("c h d t -> (h d) c t"), qk[n][:].bitcast(F32))\
                      .then_inc(qk_stored.sem, 16)

            def load_stacks(u):
                for r, (qn, kn) in enumerate(((0, 2), (1, 2), (0, 3))):
                    for stack, n in ((q_stack, qn), (k_stack, kn)):
                        sp.dma_start(stack[DH * r:DH * (r + 1), HC * u:HC * (u + 1), :].bitcast(F32),
                                     stack_dram[n, u].rearrange("h d t -> d h t"))\
                          .then_inc(stack_loaded[u].sem, 16)

            def store_max(sec, u):
                sp.wait_ge(work_free.sem, sec(work_free, (0, 4)[u] + 1))
                for r, rows in enumerate((max_hi, max_lo)):
                    sp.dma_start(q_stack[MAX_ROW + r:MAX_ROW + r + 1, HC * u:HC * (u + 1), :].bitcast(F32),
                                 rows[:].bitcast(F32))\
                      .then_inc(max_loaded[u].sem, 16)

            def batch(i, last, ahead):
                project, attend, cross = (Section(s, i, last) for s in ("project", "attend", "cross"))
                start = Section("start", i)
                if not last:
                    sp.wait_ge(stack_loaded[1].sem, start(stack_loaded[1], 0))
                    store_qk(project)
                store_max(attend, 0)
                if ahead:
                    sp.wait_ge(norm_ready.sem, project(norm_ready, 1))
                    load_x_in(i + 2)
                if not last:
                    sp.wait_ge(ctx_split.sem, attend(ctx_split, 1))
                    load_ctx(i + 1)
                store_max(attend, 1)
                if not last:
                    sp.wait_ge(qk_stored.sem, project(qk_stored, 64))
                    for u in range(2):
                        sp.wait_ge(scores_t_ready.sem, attend(scores_t_ready, 3 * HC * (u + 1)))
                        load_stacks(u)
                    sp.wait_ge(norm_ready.sem, cross(norm_ready, 1))
                    sp.wait_ge(bias_added.sem, cross(bias_added, 1))
                    load_x_res(i + 1)
                for u in range(2):
                    sp.wait_ge(work_free.sem, cross(work_free, 12 + u))
                    sp.dma_start(x2b[i, :, 2 * u:2 * u + 2, :], x_out[:, 2 * u:2 * u + 2, :])\
                      .then_inc(x2_stored.sem, 16)

            load_x_in(0)
            load_ctx(0)
            load_x_res(0)
            sec = Section("project")
            sp.wait_ge(norm_ready.sem, sec(norm_ready, 1))
            load_x_in(1)
            store_qk(sec)
            sp.wait_ge(qk_stored.sem, sec(qk_stored, 64))
            for u in range(2):
                load_stacks(u)
            with sp.Fori(0, B - 2) as i:
                batch(i, False, True)
            batch(B - 2, False, False)
            batch(B - 1, True, False)
            sp.wait_ge(x2_stored.sem, 1 + 32 * B)

        @block.gpsimd
        def _(pool):
            def rstd_of(sec):
                pool.wait_ge(var_ready.sem, sec(var_ready, 1))
                pool.sem_inc(pool_pause, 1)
                pool.tensor_scalar(rstd[:], mean_var[:, :, 1], EPS, None, ALU.add)\
                    .then_inc(eps_added.sem, 1)
                pool.wait_ge(eps_added.sem, sec(eps_added, 1))
                pool.tensor_tensor(rstd[:], rstd[:], power[:], ALU.pow).then_inc(rstd_ready.sem, 1)

            def batch(i, last):
                project, attend, cross = (Section(s, i, last) for s in ("project", "attend", "cross"))
                start = Section("start", i)
                pool.wait_ge(ctx_loaded.sem, start(ctx_loaded, 0))
                pool.sem_inc(pool_pause, 1)
                src = ctx_in[:].rearrange("p c (o m) -> p c o m", o=1).to_broadcast([P, 2, 2, M])
                dst = [t[:].rearrange("p c (o m) -> p c o m", o=2) for t in (ctx_hi, ctx_lo)]
                pool.tensor_copy(dst[0], src).then_inc(ctx_step.sem, 1)
                pool.wait_ge(ctx_step.sem, attend(ctx_step, 1))
                pool.tensor_tensor(dst[1], src, dst[0].bitcast(F32), ALU.subtract)\
                    .then_inc(ctx_split.sem, 1)
                if not last:
                    rstd_of(project)
                pool.wait_ge(work_free.sem, attend(work_free, 3))
                for half, heads in ((xk_hi, xk_hi_heads), (xk_lo, xk_lo_heads)):
                    for c in range(NC):
                        last_one = pool.tensor_tensor(
                            heads[:, c, :].rearrange("p (h m) -> p h m", h=HC),
                            half[:, c:c + 1, :].bitcast(F32).to_broadcast([P, HC, M]),
                            head_mask[:], ALU.mult)
                last_one.then_inc(heads_ready.sem, 1)
                rstd_of(cross)
                pool.wait_ge(work_free.sem, attend(work_free, 13))
                pool.wait_ge(x2_stored.sem, start(x2_stored, 0))
                pool.tensor_tensor(x_out[:], x_res[:],
                                   xo_bias[:].rearrange("p (o d) -> p o d", o=1).to_broadcast([P, NQ, D]),
                                   ALU.add).then_inc(bias_added.sem, 1)

            rstd_of(Section("project"))
            with pool.Fori(0, B - 1) as i:
                batch(i, False)
            batch(B - 1, True)

        @block.scalar
        def _(act):
            act.sem_inc(exp_done.sem, 2)
            act.sem_inc(outs_read.sem, 2)

            def hi_part(sec, n, dst, src, scale=1.0, bias=None):
                act.wait_ge(work_ready.sem, sec(work_ready, n + 1))
                if bias is not None:
                    ins = act.activation(dst, src, ACT.Identity, bias=bias, scale=1.0)
                elif scale != 1.0:
                    ins = act.mul(dst, src, scale)
                else:
                    ins = act.copy(dst, src)
                ins.then_inc(work_hi.sem, 1)

            def values(sec_v, sec_used, used):
                act.wait_ge(work_free.sem, sec_v(work_free, 8))
                if sec_used is not None:
                    act.wait_ge(probs_used.sem, sec_used(probs_used, used))
                act.copy(v_ones[:, :, :, 0:DH], v_next[:].rearrange("p q (h d) -> p q h d", d=DH))\
                   .then_inc(v_ready.sem, 1)

            def project_batch(sec):
                for c in range(NC):
                    hi_part(sec, c, feat_hi[:, c, :], work_bank(sec, c)[:])
                for n in range(4):
                    hi_part(sec, 2 + n, qk[2 * (n // 2)][:, n % 2, :], work_bank(sec, 2 + n)[:])

            def exp(sec, n, width):
                act.wait_ge(scores_t_ready.sem, sec(scores_t_ready, n + 1))
                act.wait_ge(probs_used.sem, sec(probs_used, n + 1 - NP_TILES))
                slot = (n + (3 * H if sec.name == "cross" else 0)) % NP_TILES
                act.activation(probs[slot][:, 0:width], scores_t[n % 2][:, 0:width], ACT.Exp)\
                   .then_inc(exp_done.sem, 1)

            def read_outs(sec, g, used):
                act.wait_ge(probs_used.sem, sec(probs_used, used))
                act.copy(o_ext[g % 2][:], outs[g % 2][:]).then_inc(outs_read.sem, 1)

            def back(sec):
                for c in range(NC):
                    hi_part(sec, 9 + c, feat_hi[:, c, :], work_bank(sec, 9 + c)[:])

            def batch(i, last):
                project, attend, cross = (Section(s, i, last) for s in ("project", "attend", "cross"))
                if not last:
                    project_batch(project)
                hi_part(attend, 0, max_hi[:], work_bank(attend, 0)[0:HC, :], scale=-1.0)
                for c in range(NC):
                    hi_part(attend, 1 + c, xk_hi[:, c, :], work_bank(attend, 1 + c)[:, 0:M],
                            bias=xk_bias[:, c:c + 1])
                for h in range(H):
                    if h == M1_STEP:
                        hi_part(attend, 4, max_hi[:], work_bank(attend, 4)[0:HC, :], scale=-1.0)
                    for k, width in enumerate((512, 512, 256)):
                        exp(attend, 3 * h + k, width)
                    if h % GH == 0 and h:
                        read_outs(attend, h // GH - 1, 3 * h)
                read_outs(attend, NG - 1, 3 * H)
                if not last:
                    values(project, attend, 3 * H)
                back(attend)
                for c in range(NC):
                    hi_part(cross, c, feat_hi[:, c, :], work_bank(cross, c)[:])
                if not last:
                    act.wait_ge(qk_stored.sem, project(qk_stored, 64))
                for c in range(NC):
                    hi_part(cross, 2 + c, qk[0][:, c, :], work_bank(cross, 2 + c)[:],
                            bias=xq_bias[:, c:c + 1])
                hi_part(cross, 4, xmax[0:H, :], work_bank(cross, 4)[0:H, :], scale=-1.0)
                for p in range(H // 2):
                    exp(cross, p, 512)
                    if p % 2 == 0 and p:
                        read_outs(cross, p // 2 - 1, p)
                read_outs(cross, NG - 1, H // 2)
                back(cross)

            project_batch(Section("project"))
            values(Section("project"), None, 0)
            with act.Fori(0, B - 1) as i:
                batch(i, False)
            batch(B - 1, True)

        @block.vector
        def _(dve):
            dve.sem_inc(work_free.sem, 2)
            dve.sem_inc(scores_read.sem, 2)
            steps = {"project": 0, "attend": 0, "cross": 0}

            def link(sec, ins):
                steps[sec.name] += 1
                ins.then_inc(dve_step.sem, 1)
                dve.wait_ge(dve_step.sem, sec(dve_step, steps[sec.name]))

            def layer_norm(sec, src):
                for q in range(NQ):
                    ins = dve.bn_stats(stats[:, q, :], src[:, q, :])
                link(sec, ins)
                dve.sem_inc(pause, 1)
                for q in range(NQ):
                    ins = dve.bn_aggr(mean_var[:, q, :], stats[:, q, :])
                ins.then_inc(var_ready.sem, 1)
                dve.wait_ge(rstd_ready.sem, sec(rstd_ready, 1))
                for q in range(NQ):
                    ins = dve.tensor_scalar(x_norm[:, q, :], src[:, q, :], mean_var[:, q, 0:1],
                                            rstd[:, q:q + 1], ALU.subtract, ALU.mult)
                ins.then_inc(norm_ready.sem, 1)

            def lo_part(sec, k, dst, src, hi, scale=1.0, bias=None):
                dve.wait_ge(work_hi.sem, sec(work_hi, k + 1))
                if bias is not None:
                    ins = dve.scalar_tensor_tensor(out=dst, in0=src, scalar=bias, in1=hi.bitcast(F32),
                                                   op0=ALU.add, op1=ALU.subtract)
                elif scale != 1.0:
                    ins = dve.scalar_tensor_tensor(out=dst, in0=src, scalar=scale, in1=hi.bitcast(F32),
                                                   op0=ALU.mult, op1=ALU.subtract)
                else:
                    ins = dve.tensor_tensor(dst, src, hi.bitcast(F32), ALU.subtract)
                ins.then_inc(work_free.sem, 1)

            def project_steps(sec, first):
                def feat(c):
                    return lambda: lo_part(sec, c, feat_lo[:, c, :], work_bank(sec, c)[:], feat_hi[:, c, :])

                def qk_lo(n):
                    w = 2 * (n // 2)
                    return lambda: lo_part(sec, 2 + n, qk[w + 1][:, n % 2, :], work_bank(sec, 2 + n)[:],
                                           qk[w][:, n % 2, :])

                def v_half(u):
                    def step():
                        if not first:
                            dve.wait_ge(v_ready.sem, Section("start", sec.i)(v_ready, 0))
                        dve.wait_ge(work_ready.sem, sec(work_ready, 7 + u))
                        dve.tensor_copy(v_next[:, 2 * u:2 * u + 2, :].rearrange("p q d -> p (q d)"),
                                        work_bank(sec, 6 + u)[:]).then_inc(work_free.sem, 1)
                    return step

                return [feat(0), feat(1)] + [qk_lo(n) for n in range(4)] + [v_half(u) for u in range(2)]

            def maxima(sec, h):
                for t in range(NQ):
                    n = NQ * h + t
                    w = P * (t + 1)
                    dve.wait_ge(scores_ready.sem, sec(scores_ready, n + 1))
                    dve.sem_inc(pause, 1)
                    dve.tensor_tensor_reduce(out=scratch[:, n % 2, 0:w], in0=scores[n % 2][:, 0:w],
                                             in1=row_mask[:, T - w:T], scale=1.0, scalar=LOWEST,
                                             op0=ALU.add, op1=ALU.max,
                                             accum_out=row_max[:, t, h:h + 1]).then_inc(scores_read.sem, 1)

            def normalise(sec, g):
                dve.wait_ge(work_ready.sem, sec(work_ready, 5 + g + 1))
                o = work_bank(sec, 5 + g)[:].rearrange("p (t j d) -> p t j d", t=NQ, j=GH)
                link(sec, dve.reciprocal(o_sum[:, g % 2], o[:, :, :, DH]))
                dve.tensor_tensor(
                    o_tok[:].rearrange("p t (g j d) -> p g t j d", g=NG, j=GH)[:, g],
                    o[:, :, :, 0:DH],
                    o_sum[:, g % 2].rearrange("p t (j o) -> p t j o", o=1).to_broadcast([P, NQ, GH, DH]),
                    ALU.mult).then_inc(work_free.sem, 1)

            def back(sec, k):
                for c in range(NC):
                    lo_part(sec, k + c, feat_lo[:, c, :], work_bank(sec, 9 + c)[:], feat_hi[:, c, :])

            def batch(i, last):
                project, attend, cross = (Section(s, i, last) for s in ("project", "attend", "cross"))
                start = Section("start", i)
                side = []
                if not last:
                    steps["project"] = 0
                    dve.wait_ge(x_in_loaded.sem, project(x_in_loaded, 16))
                    layer_norm(project, x_in)
                    side = project_steps(project, False)
                for h in range(HC):
                    maxima(attend, h)
                    if h and side:
                        side.pop(0)()
                        if h == 1:
                            side.pop(0)()
                for step in side:
                    step()
                lo_part(attend, 0, max_lo[:], work_bank(attend, 0)[0:HC, :], max_hi[:], scale=-1.0)
                for c in range(NC):
                    lo_part(attend, 1 + c, xk_lo[:, c, :], work_bank(attend, 1 + c)[:, 0:M],
                            xk_hi[:, c, :], bias=xk_bias[:, c:c + 1])
                dve.wait_ge(work_ready.sem, attend(work_ready, 4))
                v = work_bank(attend, 3)[:, 0:D].rearrange("p (a o d) -> p a o d", o=2, d=DH)
                vb = xv_bias[:].rearrange("p (a o d) -> p a o d", o=2, d=DH)
                dve.tensor_tensor(xv_ones[0:M, :, 0:DH], v[0:M, :, 0, :], vb[0:M, :, 0, :], ALU.add)
                dve.tensor_tensor(xv_ones[M:P, :, VW:VW + DH], v[M:P, :, 1, :], vb[M:P, :, 1, :],
                                  ALU.add).then_inc(work_free.sem, 1)
                for step in range(H + 2):
                    for h in PASS1_AT.get(step, ()):
                        maxima(attend, h)
                    if step == M1_STEP:
                        lo_part(attend, 3, max_lo[:], work_bank(attend, 4)[0:HC, :], max_hi[:], scale=-1.0)
                    if step % GH == 1 and step > 1:
                        normalise(attend, step // GH - 1)
                back(attend, 4)
                dve.wait_ge(x_res_loaded.sem, start(x_res_loaded, 0))
                for u in range(2):
                    dve.wait_ge(work_ready.sem, attend(work_ready, 12 + u))
                    r = x_res[:, 2 * u:2 * u + 2, :].rearrange("p q d -> p (q d)")
                    dve.tensor_tensor(r, work_bank(attend, 11 + u)[:], r, ALU.add)\
                       .then_inc(work_free.sem, 1)
                dve.wait_ge(work_free.sem, attend(work_free, 13))
                layer_norm(cross, x_res)
                for c in range(NC):
                    lo_part(cross, c, feat_lo[:, c, :], work_bank(cross, c)[:], feat_hi[:, c, :])
                for c in range(NC):
                    lo_part(cross, 2 + c, qk[1][:, c, :], work_bank(cross, 2 + c)[:], qk[0][:, c, :],
                            bias=xq_bias[:, c:c + 1])
                for n in range(2 * NQ):
                    dve.wait_ge(scores_ready.sem, cross(scores_ready, n + 1))
                    dve.tensor_reduce(row_max[:, n // 2, HC * (n % 2):HC * (n % 2 + 1)],
                                      scores[n % 2][:].rearrange("p (h m) -> p h m", h=HC),
                                      AX.X, ALU.max).then_inc(scores_read.sem, 1)
                lo_part(cross, 4, xmax[32:32 + H, :], work_bank(cross, 4)[0:H, :], xmax[0:H, :], scale=-1.0)
                for g in range(NG):
                    normalise(cross, g)
                back(cross, 5)
                dve.wait_ge(bias_added.sem, cross(bias_added, 1))
                for u in range(2):
                    dve.wait_ge(work_ready.sem, cross(work_ready, 12 + u))
                    r = x_out[:, 2 * u:2 * u + 2, :].rearrange("p q d -> p (q d)")
                    dve.tensor_tensor(r, work_bank(cross, 11 + u)[:], r, ALU.add)\
                       .then_inc(work_free.sem, 1)
                steps.update(attend=0, cross=0)

            sec = Section("project")
            dve.wait_ge(x_in_loaded.sem, sec(x_in_loaded, 16))
            layer_norm(sec, x_in)
            for step in project_steps(sec, True):
                step()
            with dve.Fori(0, B - 1) as i:
                batch(i, False)
            batch(B - 1, True)

        @block.tensor
        def _(pe):
            pe.sem_inc(probs_used.sem, NP_TILES)

            def fill(sec, n):
                pe.wait_ge(work_free.sem, sec(work_free, n - 1))
                return work_bank(sec, n)

            def passes(out, pairs, start=True, stop=True):
                todo = [(w, x) for (wh, wl), (xh, xl) in pairs for w, x in ((wh, xh), (wl, xh), (wh, xl))]
                for j, (w, x) in enumerate(todo):
                    ins = pe.matmul(out, w, x, start=start and j == 0, stop=stop and j == len(todo) - 1)
                return ins

            def turn(sec, n, out_rows, src):
                out = fill(sec, n)
                for t in range(NQ):
                    ins = pe.transpose(out[0:out_rows, t * P:(t + 1) * P], src(t), eye[:])
                ins.then_inc(work_ready.sem, 1)

            def feat(c, s=slice(None)):
                return feat_hi[:, c, s], feat_lo[:, c, s]

            def weight(n, c, s=slice(None)):
                return w_hi[n][:, c, s], w_lo[n][:, c, s]

            def by_features(sec, n, w, m):
                out = fill(sec, n)
                passes(out[:], [(weight(w, c, slice(m * P, (m + 1) * P)), feat(c)) for c in range(NC)])\
                    .then_inc(work_ready.sem, 1)

            def by_tokens(sec, n, w, u):
                out = fill(sec, n)
                for t in (2 * u, 2 * u + 1):
                    ins = passes(out[:, D * (t % 2):D * (t % 2 + 1)],
                                 [(feat(c, slice(t * P, (t + 1) * P)), weight(w, c)) for c in range(NC)])
                ins.then_inc(work_ready.sem, 1)

            def norm_turn(sec):
                pe.wait_ge(norm_ready.sem, sec(norm_ready, 1))
                for c in range(NC):
                    turn(sec, c, P, lambda t: x_norm[:, t, c * P:(c + 1) * P])

            def project_steps(sec):
                def q_or_k(n):
                    def step():
                        if n == 0:
                            pe.wait_ge(work_free.sem, sec(work_free, 2))
                        by_features(sec, 2 + n, "qk"[n // 2], n % 2)
                    return step
                return [lambda: norm_turn(sec)] + [q_or_k(n) for n in range(4)] \
                    + [(lambda u: lambda: by_tokens(sec, 6 + u, "v", u))(u) for u in range(2)]

            def rows(sec, h):
                for t in range(NQ):
                    n = NQ * h + t
                    pe.wait_ge(scores_read.sem, sec(scores_read, n - 1))
                    pe.matmul(scores[n % 2][:, 0:P * (t + 1)], q_stack[0:MAX_ROW, h, t * P:(t + 1) * P],
                              k_stack[0:MAX_ROW, h, 0:P * (t + 1)], start=True, stop=True)\
                      .then_inc(scores_ready.sem, 1)

            def turn_maxima(sec, n, done, lo, hi):
                pe.wait_ge(scores_read.sem, sec(scores_read, done))
                turn(sec, n, hi - lo, lambda t: row_max[:, t, lo:hi])

            def columns(sec, h, k):
                n = 3 * h + k
                pe.wait_ge(exp_done.sem, sec(exp_done, n - 1))
                bank = scores_t[n % 2]
                for kt, col, w in PARTS[k]:
                    pe.matmul(bank[:, col:col + w], k_stack[0:MAX_ROW + 2, h, kt * P:(kt + 1) * P],
                              q_stack[0:MAX_ROW + 2, h, kt * P:T], start=True, stop=False)
                    ins = pe.matmul(bank[:, col:col + P], eye_bf[:], tri_bf[:], start=False, stop=True)
                ins.then_inc(scores_t_ready.sem, 1)

            def weigh(sec, h, k):
                n = 3 * h + k
                pe.wait_ge(exp_done.sem, sec(exp_done, n + 1))
                g, j = h // GH, h % GH
                if j == 0 and k == 0:
                    pe.wait_ge(outs_read.sem, sec(outs_read, g - 1))
                for kt, col, w in PARTS[k]:
                    ins = pe.matmul(outs[g % 2][VW * j:VW * (j + 1), kt * P:T], v_ones[:, kt, h, :],
                                    probs[n % NP_TILES][:, col:col + w], start=(k == 0), stop=(kt == 2),
                                    tile_position=(0, VW * j))
                ins.then_inc(probs_used.sem, 1)

            def turn_outs(sec, g):
                pe.wait_ge(outs_read.sem, sec(outs_read, g + 1))
                turn(sec, 5 + g, P, lambda t: o_ext[g % 2][:, t * P:(t + 1) * P])

            def finish(sec, w):
                pe.wait_ge(work_free.sem, sec(work_free, 9))
                for c in range(NC):
                    turn(sec, 9 + c, P, lambda t: o_tok[:, t, c * P:(c + 1) * P])
                pe.wait_ge(work_free.sem, sec(work_free, 11))
                for u in range(2):
                    by_tokens(sec, 11 + u, w, u)

            def batch(i, last):
                project, attend, cross = (Section(s, i, last) for s in ("project", "attend", "cross"))
                start = Section("start", i)
                side = [] if last else project_steps(project)
                pe.wait_ge(stack_loaded[0].sem, start(stack_loaded[0], 0))
                for h in range(HC):
                    rows(attend, h)
                    if h and side:
                        side.pop(0)()
                for step in side:
                    step()
                turn_maxima(attend, 0, NQ * HC, 0, HC)
                pe.wait_ge(ctx_split.sem, attend(ctx_split, 1))
                for m in range(NC):
                    out = fill(attend, 1 + m)
                    passes(out[:, 0:M], [(weight("xk", c, slice(m * P, (m + 1) * P)),
                                          (ctx_hi[:, c, 0:M], ctx_lo[:, c, 0:M])) for c in range(2)])\
                        .then_inc(work_ready.sem, 1)
                out = fill(attend, 3)
                passes(out[:, 0:D], [((ctx_hi[:, c, :], ctx_lo[:, c, :]), weight("xv", c))
                                     for c in range(2)]).then_inc(work_ready.sem, 1)
                pe.wait_ge(stack_loaded[1].sem, start(stack_loaded[1], 0))
                for step in range(H + 2):
                    for h in PASS1_AT.get(step, ()):
                        rows(attend, h)
                    if step == M1_STEP:
                        turn_maxima(attend, 4, NQ * H, HC, H)
                    if step % HC == 0 and step < H:
                        pe.wait_ge(max_loaded[step // HC].sem, attend(max_loaded[step // HC], 32))
                    if step == 1:
                        pe.wait_ge(v_ready.sem, start(v_ready, 0))
                    for k in range(3):
                        if step < H:
                            columns(attend, step, k)
                        if 1 <= step <= H:
                            weigh(attend, step - 1, k)
                    if step % GH == 1 and step > 1:
                        turn_outs(attend, step // GH - 1)
                finish(attend, "p")

                norm_turn(cross)
                pe.wait_ge(work_free.sem, cross(work_free, 2))
                for m in range(NC):
                    by_features(cross, 2 + m, "xq", m)
                pe.wait_ge(work_free.sem, cross(work_free, 4))
                pe.wait_ge(heads_ready.sem, attend(heads_ready, 1))
                for n in range(2 * NQ):
                    t, c = n // 2, n % 2
                    pe.wait_ge(scores_read.sem, cross(scores_read, n - 1))
                    pe.matmul(scores[n % 2][:], qk[0][:, c, t * P:(t + 1) * P], xk_hi_heads[:, c, :],
                              start=True, stop=True).then_inc(scores_ready.sem, 1)
                turn_maxima(cross, 4, 2 * NQ, 0, H)
                pe.wait_ge(work_free.sem, cross(work_free, 5))
                for p in range(H // 2 + 1):
                    if p < H // 2:
                        pe.wait_ge(exp_done.sem, cross(exp_done, p - 1))
                        c, s = p // GH, slice((p % GH) * P, (p % GH + 1) * P)
                        passes(scores_t[p % 2][:], [((xk_hi_heads[:, c, s], xk_lo_heads[:, c, s]),
                                                     (qk[0][:, c, :], qk[1][:, c, :]))], stop=False)
                        pe.matmul(scores_t[p % 2][:], pick_max[:, p, :], xmax[:], start=False, stop=True)\
                          .then_inc(scores_t_ready.sem, 1)
                    if p:
                        n, g = p - 1, (p - 1) // 2
                        pe.wait_ge(exp_done.sem, cross(exp_done, n + 1))
                        if n % 2 == 0:
                            pe.wait_ge(outs_read.sem, cross(outs_read, g - 1))
                        base = 2 * VW * (n % 2)
                        pe.matmul(outs[g % 2][base:base + 2 * VW, :], xv_ones[:, n, :],
                                  probs[(3 * H + n) % NP_TILES][:], start=True, stop=True,
                                  tile_position=(0, base)).then_inc(probs_used.sem, 1)
                    if p >= 4 and p % 2 == 0:
                        turn_outs(cross, p // 2 - 2)
                turn_outs(cross, NG - 1)
                finish(cross, "xo")

            for step in project_steps(Section("project")):
                step()
            with pe.Fori(0, B - 1) as i:
                batch(i, False)
            batch(B - 1, True)


class Count:

    def __init__(self, sem, per, first=0):
        self.sem, self.per, self.first = sem, per, first

    def at(self, i, n):
        return self.per * i + (self.first + n)


def mixture(nc, a, x2_dram, out):
    ctx = ExitStack()
    with ctx:
        def sb(name, shape, dt=F32):
            return ctx.enter_context(nc.sbuf_tensor(name, shape, dt))

        def bank(name):
            return ctx.enter_context(nc.psum_tensor(name, [P, 512], F32))

        def sem(name):
            return ctx.enter_context(nc.semaphore(name))

        up_hi = sb("up_hi", [P, NE, NC, 2 * HID], F32R)
        up_lo = sb("up_lo", [P, NE, NC, 2 * HID], F32R)
        down_hi = sb("down_hi", [P, NE, HID // P, D], F32R)
        down_lo = sb("down_lo", [P, NE, HID // P, D], F32R)
        router_in = sb("router_in", [P, NC, E])
        router_hi = sb("router_hi", [P, NC, E], F32R)
        router_lo = sb("router_lo", [P, NC, E], F32R)
        expert_bias = sb("expert_bias", [P, E])
        expert_no = sb("expert_no", [P, E])
        eye = sb("f_eye", [P, P])
        power = sb("f_power", [P, NQ])
        raw_up = [sb(f"raw_up{n}", [P, NC, 2 * HID]) for n in range(2)]
        raw_down = [sb(f"raw_down{n}", [P, HID // P, D]) for n in range(2)]

        x_in = sb("f_x_in", [P, NQ, D])
        x_res = sb("f_x_res", [P, NQ, D])
        x_norm = sb("f_x_norm", [P, NQ, D])
        y_out = sb("y_out", [P, NQ, D])
        stats = sb("f_stats", [P, NQ, 6])
        mean_var = sb("f_mean_var", [P, NQ, 2])
        rstd = sb("f_rstd", [P, NQ])
        feat_hi = sb("f_feat_hi", [P, NC, T], F32R)
        feat_lo = sb("f_feat_lo", [P, NC, T], F32R)
        logits = sb("logits", [P, NQ, E])
        top_logit = sb("top_logit", [P, NQ])
        weight_sum = sb("weight_sum", [P, NQ])
        weights = sb("weights", [P, NQ, E])
        biased = sb("biased", [P, NQ, E])
        top = sb("top", [P, NQ, 8])
        top_at = sb("top_at", [P, NQ, 8], U32)
        top_no = sb("top_no", [P, NQ, 8])
        chosen = sb("chosen", [P, 2, NQ, E])
        gates = sb("gates", [P, NQ, NE])
        tanh = [sb(f"tanh{n}", [P, HID]) for n in range(2)]
        gated = [sb(f"gated{n}", [P, HID]) for n in range(2)]
        hidden = [sb(f"hidden{n}", [P, HID]) for n in range(2)]
        hid_hi = [sb(f"hid_hi{n}", [P, HID], F32R) for n in range(2)]
        hid_lo = [sb(f"hid_lo{n}", [P, HID], F32R) for n in range(2)]

        ups = [bank(f"ups{n}") for n in range(2)]
        turned = [bank(f"turned{n}") for n in range(2)]
        downs = [bank(f"downs{n}") for n in range(2)]
        work = [bank(f"f_work{n}") for n in range(2)]

        G = B
        U = NQ * NE
        w_loaded = [sem(f"f_w_loaded{n}") for n in range(2)]
        w_hi_done = sem("f_w_hi_done")
        w_lo_done = sem("f_w_lo_done")
        c_loaded = sem("f_c_loaded")
        prep_step = sem("f_prep_step")
        gate_step = sem("f_gate_step")
        pause, pool_pause = sem("f_pause"), sem("f_pool_pause")
        x_in_loaded = Count(sem("f_x_in_loaded"), 16)
        x_res_loaded = Count(sem("f_x_res_loaded"), 16)
        var_ready = Count(sem("f_var_ready"), 1)
        eps_added = Count(sem("f_eps_added"), 1)
        rstd_ready = Count(sem("f_rstd_ready"), 1)
        norm_ready = Count(sem("f_norm_ready"), 1)
        work_ready = Count(sem("f_work_ready"), 3)
        work_hi = Count(sem("f_work_hi"), 2)
        work_free = Count(sem("f_work_free"), 3, 2)
        weighed = Count(sem("weighed"), 1)
        gates_ready = Count(sem("gates_ready"), 1)
        ups_ready = Count(sem("ups_ready"), U)
        tanh_done = Count(sem("tanh_done"), U)
        ups_free = Count(sem("ups_free"), U, 2)
        turned_ready = Count(sem("turned_ready"), U)
        hid_hi_done = Count(sem("hid_hi_done"), U)
        hid_ready = Count(sem("hid_ready"), U, 2)
        downs_ready = Count(sem("downs_ready"), U)
        downs_free = Count(sem("downs_free"), NQ, 2)
        dve_step = Count(sem("f_dve_step"), U + 11)
        stored = Count(sem("f_stored"), 16, 1)

        xg = x2_dram.rearrange("b (q p) d -> b p q d", p=P)
        og = out.rearrange("b (q p) d -> b p q d", p=P)

        block = ctx.enter_context(nc.Block())

        @block.sync
        def _(sp):
            sp.sem_inc(stored.sem, 1)
            sp.dma_start(eye[:], a["eye"]).then_inc(c_loaded, 16)
            sp.dma_start(router_in[:], a["router_w"].rearrange("(c p) e -> p c e", p=P)).then_inc(c_loaded, 16)
            sp.dma_start(expert_bias[:], a["expert_bias"]).then_inc(c_loaded, 16)
            sp.dma_start(expert_no[:], a["expert_no"]).then_inc(c_loaded, 16)
            sp.dma_start(x_in[:], xg[0]).then_inc(x_in_loaded.sem, 16)
            for e in range(NE):
                if e >= 2:
                    sp.wait_ge(w_lo_done, e - 1)
                sp.dma_start(raw_up[e % 2][:], a["w_up"][e].rearrange("(c p) n -> p c n", p=P))\
                  .then_inc(w_loaded[e % 2], 16)
                sp.dma_start(raw_down[e % 2][:], a["w_down"][e].rearrange("(c p) n -> p c n", p=P))\
                  .then_inc(w_loaded[e % 2], 16)

            def group(g, ahead):
                sp.wait_ge(stored.sem, stored.at(g, 0))
                sp.dma_start(x_res[:], xg[g]).then_inc(x_res_loaded.sem, 16)
                if ahead:
                    sp.wait_ge(norm_ready.sem, norm_ready.at(g, 1))
                    sp.dma_start(x_in[:], xg[g + 1]).then_inc(x_in_loaded.sem, 16)
                sp.wait_ge(downs_free.sem, downs_free.at(g, NQ))
                sp.dma_start(og[g], y_out[:]).then_inc(stored.sem, 16)

            with sp.Fori(0, G - 1) as g:
                group(g, True)
            group(G - 1, False)
            sp.wait_ge(stored.sem, stored.at(G, 0))

        @block.gpsimd
        def _(pool):
            pool.memset(power[:], -0.5)
            pool.memset(gates[:, :, E:NE], 0.5).then_inc(gate_step, 1)
            with pool.Fori(0, G) as g:
                pool.wait_ge(var_ready.sem, var_ready.at(g, 1))
                pool.sem_inc(pool_pause, 1)
                pool.tensor_scalar(rstd[:], mean_var[:, :, 1], EPS, None, ALU.add)\
                    .then_inc(eps_added.sem, 1)
                pool.wait_ge(eps_added.sem, eps_added.at(g, 1))
                pool.tensor_tensor(rstd[:], rstd[:], power[:], ALU.pow).then_inc(rstd_ready.sem, 1)

        @block.scalar
        def _(act):
            for e in range(NE):
                act.wait_ge(w_loaded[e % 2], 32 * (e // 2 + 1))
                act.copy(up_hi[:, e], raw_up[e % 2][:])
                act.copy(down_hi[:, e], raw_down[e % 2][:]).then_inc(w_hi_done, 1)

            with act.Fori(0, G) as g:
                for c in range(NC):
                    act.wait_ge(work_ready.sem, work_ready.at(g, c + 1))
                    act.copy(feat_hi[:, c, :], work[c][:]).then_inc(work_hi.sem, 1)
                act.wait_ge(work_free.sem, work_free.at(g, 3))
                act.activation(weights[:], logits[:], ACT.Exp).then_inc(weighed.sem, 1)
                for u in range(U + 1):
                    if u < U:
                        act.wait_ge(ups_ready.sem, ups_ready.at(g, u + 1))
                        act.activation(tanh[u % 2][:], ups[u % 2][:, 0:HID], ACT.Tanh, scale=0.5)\
                           .then_inc(tanh_done.sem, 1)
                    if u:
                        act.wait_ge(turned_ready.sem, turned_ready.at(g, u))
                        act.copy(hid_hi[(u - 1) % 2][:], turned[(u - 1) % 2][:, 0:HID])\
                           .then_inc(hid_hi_done.sem, 1)

        @block.vector
        def _(dve):
            dve.sem_inc(work_free.sem, 2)
            dve.sem_inc(ups_free.sem, 2)
            dve.sem_inc(hid_ready.sem, 2)
            dve.sem_inc(downs_free.sem, 2)
            dve.wait_ge(c_loaded, 16 * 4)
            dve.wait_ge(gate_step, 1)
            dve.tensor_copy(router_hi[:], router_in[:]).then_inc(prep_step, 1)
            dve.wait_ge(prep_step, 1)
            dve.tensor_tensor(router_lo[:], router_in[:], router_hi[:].bitcast(F32), ALU.subtract)
            for e in range(NE):
                dve.wait_ge(w_hi_done, e + 1)
                dve.tensor_tensor(up_lo[:, e], raw_up[e % 2][:], up_hi[:, e].bitcast(F32), ALU.subtract)
                dve.tensor_tensor(down_lo[:, e], raw_down[e % 2][:], down_hi[:, e].bitcast(F32),
                                  ALU.subtract).then_inc(w_lo_done, 1)

            with dve.Fori(0, G) as g:
                steps = [0]

                def link(ins):
                    steps[0] += 1
                    ins.then_inc(dve_step.sem, 1)
                    dve.wait_ge(dve_step.sem, dve_step.at(g, steps[0]))

                def spread(t):
                    return t.rearrange("p (q o) -> p q o", o=1).to_broadcast([P, NQ, E])

                dve.wait_ge(x_in_loaded.sem, x_in_loaded.at(g, 16))
                for q in range(NQ):
                    ins = dve.bn_stats(stats[:, q, :], x_in[:, q, :])
                link(ins)
                dve.sem_inc(pause, 1)
                for q in range(NQ):
                    ins = dve.bn_aggr(mean_var[:, q, :], stats[:, q, :])
                ins.then_inc(var_ready.sem, 1)
                dve.wait_ge(rstd_ready.sem, rstd_ready.at(g, 1))
                for q in range(NQ):
                    ins = dve.tensor_scalar(x_norm[:, q, :], x_in[:, q, :], mean_var[:, q, 0:1],
                                            rstd[:, q:q + 1], ALU.subtract, ALU.mult)
                ins.then_inc(norm_ready.sem, 1)
                for c in range(NC):
                    dve.wait_ge(work_hi.sem, work_hi.at(g, c + 1))
                    dve.tensor_tensor(feat_lo[:, c, :], work[c][:], feat_hi[:, c, :].bitcast(F32),
                                      ALU.subtract).then_inc(work_free.sem, 1)
                dve.wait_ge(work_ready.sem, work_ready.at(g, 3))
                lg = work[0][:, 0:NQ * E].rearrange("p (q e) -> p q e", e=E)
                link(dve.tensor_reduce(top_logit[:], lg, AX.X, ALU.max))
                dve.tensor_tensor(logits[:], lg, spread(top_logit[:]), ALU.subtract)\
                    .then_inc(work_free.sem, 1)
                dve.wait_ge(weighed.sem, weighed.at(g, 1))
                link(dve.tensor_reduce(weight_sum[:], weights[:], AX.X, ALU.add))
                link(dve.reciprocal(weight_sum[:], weight_sum[:]))
                link(dve.tensor_tensor(weights[:], weights[:], spread(weight_sum[:]), ALU.mult))
                link(dve.tensor_tensor(
                    biased[:], weights[:],
                    expert_bias[:].rearrange("p (o e) -> p o e", o=1).to_broadcast([P, NQ, E]), ALU.add))
                dve.sem_inc(pause, 1)
                for q in range(NQ):
                    ins = dve.max(top[:, q, :], biased[:, q, :])
                link(ins)
                dve.sem_inc(pause, 1)
                for q in range(NQ):
                    ins = dve.max_index(top_at[:, q, :], top[:, q, :], biased[:, q, :])
                link(ins)
                link(dve.tensor_copy(top_no[:], top_at[:]))
                for k in range(2):
                    ins = dve.tensor_tensor(
                        chosen[:, k], expert_no[:].rearrange("p (o e) -> p o e", o=1).to_broadcast([P, NQ, E]),
                        top_no[:, :, k:k + 1].to_broadcast([P, NQ, E]), ALU.is_equal)
                link(ins)
                link(dve.tensor_tensor(chosen[:, 0], chosen[:, 0], chosen[:, 1], ALU.add))
                dve.scalar_tensor_tensor(out=gates[:, :, 0:E], in0=chosen[:, 0], scalar=0.5,
                                         in1=weights[:], op0=ALU.mult, op1=ALU.mult)\
                    .then_inc(gates_ready.sem, 1)
                dve.wait_ge(gates_ready.sem, gates_ready.at(g, 1))
                dve.wait_ge(x_res_loaded.sem, x_res_loaded.at(g, 16))
                for u in range(U + 2):
                    if u < U:
                        t, e = u // NE, u % NE
                        dve.wait_ge(tanh_done.sem, tanh_done.at(g, u + 1))
                        link(dve.scalar_tensor_tensor(out=gated[u % 2][:], in0=tanh[u % 2][:], scalar=1.0,
                                                      in1=ups[u % 2][:, 0:HID], op0=ALU.add, op1=ALU.mult))
                        dve.scalar_tensor_tensor(out=hidden[u % 2][:], in0=gated[u % 2][:],
                                                 scalar=gates[:, t, e:e + 1], in1=ups[u % 2][:, HID:2 * HID],
                                                 op0=ALU.mult, op1=ALU.mult).then_inc(ups_free.sem, 1)
                    if 1 <= u <= U:
                        v = u - 1
                        dve.wait_ge(hid_hi_done.sem, hid_hi_done.at(g, v + 1))
                        dve.tensor_tensor(hid_lo[v % 2][:], turned[v % 2][:, 0:HID],
                                          hid_hi[v % 2][:].bitcast(F32), ALU.subtract)\
                            .then_inc(hid_ready.sem, 1)
                    if u >= 2 and (u - 2) % NE == NE - 1:
                        t = (u - 2) // NE
                        if t == 0:
                            dve.wait_ge(stored.sem, stored.at(g, 0))
                        dve.wait_ge(downs_ready.sem, downs_ready.at(g, u - 1))
                        dve.tensor_tensor(y_out[:, t, :], downs[t % 2][:, 0:D], x_res[:, t, :], ALU.add)\
                            .then_inc(downs_free.sem, 1)
                assert steps[0] == dve_step.per, steps

        @block.tensor
        def _(pe):
            def passes(out, pairs, start=True, stop=True):
                todo = [(w, x) for (wh, wl), (xh, xl) in pairs for w, x in ((wh, xh), (wl, xh), (wh, xl))]
                for j, (w, x) in enumerate(todo):
                    ins = pe.matmul(out, w, x, start=start and j == 0, stop=stop and j == len(todo) - 1)
                return ins

            def feat(c, t):
                return feat_hi[:, c, t * P:(t + 1) * P], feat_lo[:, c, t * P:(t + 1) * P]

            pe.wait_ge(c_loaded, 16 * 4)
            pe.wait_ge(w_lo_done, NE)
            with pe.Fori(0, G) as g:
                pe.wait_ge(norm_ready.sem, norm_ready.at(g, 1))
                pe.wait_ge(work_free.sem, work_free.at(g, 0))
                for c in range(NC):
                    for t in range(NQ):
                        ins = pe.transpose(work[c][:, t * P:(t + 1) * P],
                                           x_norm[:, t, c * P:(c + 1) * P], eye[:])
                    ins.then_inc(work_ready.sem, 1)
                pe.wait_ge(work_free.sem, work_free.at(g, 2))
                for t in range(NQ):
                    ins = passes(work[0][:, E * t:E * (t + 1)],
                                 [(feat(c, t), (router_hi[:, c, :], router_lo[:, c, :])) for c in range(NC)])
                ins.then_inc(work_ready.sem, 1)

                for u in range(U + 2):
                    if u < U:
                        t, e = u // NE, u % NE
                        pe.wait_ge(ups_free.sem, ups_free.at(g, u - 1))
                        passes(ups[u % 2][:], [(feat(c, t), (up_hi[:, e, c, :], up_lo[:, e, c, :]))
                                               for c in range(NC)]).then_inc(ups_ready.sem, 1)
                    if 1 <= u <= U:
                        v = u - 1
                        pe.wait_ge(ups_free.sem, ups_free.at(g, v + 1))
                        pe.wait_ge(hid_ready.sem, hid_ready.at(g, v - 1))
                        for c in range(HID // P):
                            ins = pe.transpose(turned[v % 2][:, c * P:(c + 1) * P],
                                               hidden[v % 2][:, c * P:(c + 1) * P], eye[:])
                        ins.then_inc(turned_ready.sem, 1)
                    if u >= 2:
                        v = u - 2
                        t, e = v // NE, v % NE
                        pe.wait_ge(hid_ready.sem, hid_ready.at(g, v + 1))
                        if e == 0:
                            pe.wait_ge(downs_free.sem, downs_free.at(g, t - 1))
                        passes(downs[t % 2][:, 0:D],
                               [((hid_hi[v % 2][:, c * P:(c + 1) * P], hid_lo[v % 2][:, c * P:(c + 1) * P]),
                                 (down_hi[:, e, c, :], down_lo[:, e, c, :])) for c in range(HID // P)],
                               start=e == 0, stop=e == NE - 1).then_inc(downs_ready.sem, 1)


def constants():
    start = 2.0 ** (-2.0 ** (-(np.log2(H) - 3)))
    slopes = np.array([start * start ** i for i in range(H)], np.float32)
    bias = -(slopes[:, None] * np.arange(T, dtype=np.float32)[None, :]).astype(np.float32)
    hi = (bias.view(np.uint32) & np.uint32(0xFFFFF000)).view(np.float32)
    alibi = np.stack([hi, bias - hi]).reshape(2, H // 2, NQ, D)
    k = np.arange(P)
    tri = np.where(k[:, None] > k[None, :], MASKED, 0.0).astype(np.float32)
    row_mask = np.zeros((P, T), np.float32)
    row_mask[:, T - P:] = tri.T
    head_mask = np.repeat((k[:, None] // DH == np.arange(HC)[None, :])[:, :, None], M, 2)
    pick = np.zeros((2 * 32, H // 2, P), np.float32)
    for h in range(H):
        for r in (h, 32 + h):
            pick[r, h // 2, M * (h % 2):M * (h % 2 + 1)] = 1.0
    return {"eye": np.eye(P, dtype=np.float32), "tri": tri, "row_mask": row_mask,
            "head_mask": head_mask.astype(np.float32), "pick_max": pick.reshape(2 * 32, NQ, D),
            "alibi": alibi, "expert_no": np.tile(np.arange(E, dtype=np.float32), (P, 1))}


def layouts(v):
    kv = v["L0_xattn_Wkv"].reshape(H, 2, DH, DC)
    bkv = v["L0_xattn_bkv"].reshape(H, 2, DH)
    ups = [np.concatenate([w1, w3], -1) for w1, w3 in zip(v["L0_ffn_w1"], v["L0_ffn_w3"])]
    ups.append(np.concatenate([v["L0_ffn_sw1"], v["L0_ffn_sw3"]], -1))
    d = {"x": v["x"], "ctx": v["ctx_768"].transpose(0, 2, 1),
         "w_xk": kv[:, 0].reshape(D, DC).T, "w_xv": kv[:, 1].reshape(D, DC).T,
         "w_xq": v["L0_xattn_Wq"].T, "w_xo": v["L0_xattn_Wo"].T, "w_p": v["L0_attn_Wp"].T,
         "xq_bias": v["L0_xattn_bq"].reshape(NC, P).T, "xk_bias": bkv[:, 0].reshape(NC, P).T,
         "xv_bias": np.broadcast_to(bkv[:, 1].reshape(1, D), (P, D)),
         "xo_bias": np.broadcast_to(v["L0_xattn_bo"], (P, D)),
         "w_up": np.stack(ups),
         "w_down": np.concatenate([v["L0_ffn_w2"], v["L0_ffn_sw2"][None]], 0),
         "router_w": v["L0_ffn_router_w"],
         "expert_bias": np.broadcast_to(v["L0_ffn_expert_bias"], (P, E))}
    for n in "qkv":
        d["w_" + n] = v["L0_attn_W" + n].T
        d["a_" + n] = v["L0_attn_A" + n].T
        d["b_" + n] = v["L0_attn_B" + n]
    return d


def kernel(**inputs):
    import concourse.bacc as bacc
    from concourse.bass_utils import run_bass_kernel_spmd

    nc = bacc.Bacc("TRN2", target_bir_lowering=False, num_devices=1)
    arrays, aps = {}, {}
    host = {**layouts({k: np.asarray(v) for k, v in inputs.items()}), **constants()}
    for name, value in host.items():
        arrays["in_" + name] = np.ascontiguousarray(value)
        aps[name] = nc.dram_tensor("in_" + name, value.shape, F32, kind="ExternalInput").ap()
    out = nc.dram_tensor("out", (B, T, D), F32, kind="ExternalOutput").ap()
    x2 = nc.dram_tensor("x2", (B, T, D), F32, kind="Internal").ap()
    attention(nc, aps, x2)
    mixture(nc, aps, x2, out)
    r = run_bass_kernel_spmd(nc, [arrays], core_ids=[0])
    return r.results[0]["out"]
```

```python
from contextlib import ExitStack

import numpy as np

import concourse.bass as bass
from concourse import mybir

F32 = mybir.dt.float32
F32R = mybir.dt.float32r
BF16 = mybir.dt.bfloat16
U32 = mybir.dt.uint32
ALU = mybir.AluOpType
ACT = mybir.ActivationFunctionType
AX = mybir.AxisListType

P = 128
B, T, D = 16, 512, 256
H, DH = 16, 16
M, DC = 64, 192
R = 8
E, HID = 8, 256
NE = E + 1
EPS = 1e-5
NQ = T // P
NC = D // P
HC = H // NC
GH = 4
VW = 32
NG = H // GH
NP_TILES = 7
ONES_ROW, BIAS_ROW, MAX_ROW = 64, 64, 96
MASKED = -1.0e30
LOWEST = -3.0e38

PARTS = [[(0, 0, 512)], [(1, 0, 384), (3, 384, 128)], [(2, 0, 256)]]

PASS1_AT = {0: (8, 9), 1: (10, 11), 2: (12,), 3: (13,), 4: (14, 15)}
M1_STEP = 5
DVE_STEPS = (1, NG, 1 + NG)


class Signal:

    def __init__(self, sem, project=0, attend=0, cross=0, first=0):
        self.sem, self.first = sem, first
        self.per = {"project": project, "attend": attend, "cross": cross}


class Section:

    def __init__(self, name, i=None, last=False):
        self.name, self.i, self.last = name, i, last

    def __call__(self, signal, n):
        per = signal.per
        value = signal.first + n
        if self.i is None:
            return value
        value += per["project"]
        if self.name in ("attend", "cross") and not self.last:
            value += per["project"]
        if self.name == "cross":
            value += per["attend"]
        return self.i * sum(per.values()) + value


def attention(nc, a, x2_dram):
    ctx = ExitStack()
    with ctx:
        def sb(name, shape, dt=F32):
            return ctx.enter_context(nc.sbuf_tensor(name, shape, dt))

        def bank(name):
            return ctx.enter_context(nc.psum_tensor(name, [P, 512], F32))

        def sem(name):
            return ctx.enter_context(nc.semaphore(name))

        eye = sb("eye", [P, P])
        eye_bf = sb("eye_bf", [P, P], BF16)
        tri_bf = sb("tri_bf", [P, P], BF16)
        row_mask = sb("row_mask", [P, T])
        head_mask = sb("head_mask", [P, HC, M])
        pick_max = sb("pick_max", [2 * 32, H // 2, P], F32R)
        power = sb("power", [P, NQ])
        names = ("q", "k", "v", "p", "xq", "xk", "xv", "xo")
        w_hi = {n: sb(f"w_{n}_hi", [P, NC, D], F32R) for n in names}
        w_lo = {n: sb(f"w_{n}_lo", [P, NC, D], F32R) for n in names}
        xq_bias = sb("xq_bias", [P, NC])
        xk_bias = sb("xk_bias", [P, NC])
        xv_bias = sb("xv_bias", [P, D])
        xo_bias = sb("xo_bias", [P, D])

        q_stack = sb("q_stack", [P, H, T], F32R)
        k_stack = sb("k_stack", [P, H, T], F32R)
        x_in = sb("x_in", [P, NQ, D])
        x_norm = sb("x_norm", [P, NQ, D])
        x_res = sb("x_res", [P, NQ, D])
        x_out = sb("x_out", [P, NQ, D])
        stats = sb("stats", [P, NQ, 6])
        mean_var = sb("mean_var", [P, NQ, 2])
        rstd = sb("rstd", [P, NQ])
        feat_hi = sb("feat_hi", [P, NC, T], F32R)
        feat_lo = sb("feat_lo", [P, NC, T], F32R)
        qk = [sb(f"qk{n}", [P, NC, T], F32R) for n in range(4)]
        v_next = sb("v_next", [P, NQ, D])
        v_ones = sb("v_ones", [P, NQ, H, VW])
        scratch = sb("scratch", [P, 2, T])
        row_max = sb("row_max", [P, NQ, H])
        max_hi = sb("max_hi", [HC, T], F32R)
        max_lo = sb("max_lo", [HC, T], F32R)
        xmax = sb("xmax", [2 * 32, T], F32R)
        probs = [sb(f"probs{n}", [P, T]) for n in range(NP_TILES)]
        o_ext = [sb(f"o_ext{n}", [P, T]) for n in range(2)]
        o_sum = sb("o_sum", [P, 2, NQ, GH])
        o_tok = sb("o_tok", [P, NQ, D])
        ctx_in = sb("ctx_in", [P, 2, M])
        ctx_hi = sb("ctx_hi", [P, 2, 2 * M], F32R)
        ctx_lo = sb("ctx_lo", [P, 2, 2 * M], F32R)
        xk_hi = sb("xk_hi", [P, NC, M], F32R)
        xk_lo = sb("xk_lo", [P, NC, M], F32R)
        xk_hi_heads = sb("xk_hi_heads", [P, NC, HC * M], F32R)
        xk_lo_heads = sb("xk_lo_heads", [P, NC, HC * M], F32R)
        xv_ones = sb("xv_ones", [P, H // 2, 2 * VW])

        scores = [bank(f"scores{n}") for n in range(2)]
        scores_t = [bank(f"scores_t{n}") for n in range(2)]
        outs = [bank(f"outs{n}") for n in range(2)]
        work = [bank(f"work{n}") for n in range(2)]

        stack_dram = nc.dram_tensor("stack_dram", (4, NC, HC, DH, T), F32, kind="Internal").ap()

        w_loaded = sem("w_loaded")
        c_loaded = sem("c_loaded")
        lora_ready = sem("lora_ready")
        zeroed = sem("zeroed")
        pool_step = sem("pool_step")
        prep_step = sem("prep_step")
        alibi_loaded = [sem(f"alibi_loaded{n}") for n in range(2)]
        alibi_used = sem("alibi_used")
        raw = {n: (x_in, x_norm, x_res, x_out)[j // 2][:, 2 * (j % 2):2 * (j % 2) + 2, :]
               for j, n in enumerate(names)}
        with ExitStack() as prep:
            def tmp(name, shape, dt=F32):
                return prep.enter_context(nc.sbuf_tensor(name, shape, dt))

            lora_a = {n: probs[j][0:R, 0:D] for j, n in enumerate(("q", "k", "v"))}
            lora_b = {n: probs[j][0:R, D:2 * D] for j, n in enumerate(("q", "k", "v"))}
            alibi = (v_next, o_tok)
            block = prep.enter_context(nc.Block())

            @block.sync
            def _(sp):
                for n in names:
                    src = a["w_" + n]
                    if src.shape[0] == D:
                        sp.dma_start(raw[n], src.rearrange("(c p) n -> p c n", p=P)).then_inc(w_loaded, 16)
                sp.wait_ge(zeroed, 1)
                for n in ("xk", "xv"):
                    sp.dma_start(raw[n][:, 0, :], a["w_" + n][0:P, :]).then_inc(w_loaded, 16)
                    sp.dma_start(raw[n][0:DC - P, 1, :], a["w_" + n][P:DC, :]).then_inc(w_loaded, 16)
                for n in ("q", "k", "v"):
                    sp.dma_start(lora_a[n], a["a_" + n]).then_inc(w_loaded, 16)
                    sp.dma_start(lora_b[n], a["b_" + n]).then_inc(w_loaded, 16)
                for dst, src in ((eye, "eye"), (row_mask, "row_mask"), (xv_bias, "xv_bias"),
                                 (xo_bias, "xo_bias"), (xq_bias, "xq_bias"), (xk_bias, "xk_bias")):
                    sp.dma_start(dst[:], a[src]).then_inc(c_loaded, 16)
                sp.dma_start(head_mask[:], a["head_mask"]).then_inc(c_loaded, 16)
                sp.dma_start(scratch[:, 0, 0:P], a["tri"]).then_inc(c_loaded, 16)
                sp.dma_start(o_tok[0:2 * 32, :, :], a["pick_max"]).then_inc(c_loaded, 16)
                for part in range(H // 2):
                    sp.wait_ge(alibi_used, max(part - 1, 0) + 2)
                    sp.dma_start(alibi[part % 2][BIAS_ROW:BIAS_ROW + 2, :, :], a["alibi"][:, part])\
                      .then_inc(alibi_loaded[part % 2], 16)

            @block.tensor
            def _(pe):
                pe.wait_ge(w_loaded, 16 * 16)
                for j, n in enumerate(("q", "k", "v")):
                    for c in range(NC):
                        pe.matmul((scores + scores_t + outs)[2 * j + c][:, 0:D],
                                  lora_b[n][:, c * P:(c + 1) * P], lora_a[n][:, :],
                                  start=True, stop=True).then_inc(lora_ready, 1)

            @block.gpsimd
            def _(pool):
                pool.memset(raw["xk"][:, 1, :], 0.0)
                pool.memset(raw["xv"][:, 1, :], 0.0).then_inc(zeroed, 1)
                pool.memset(ctx_in[:], 0.0)
                pool.memset(power[:], -0.5)
                pool.memset(v_ones[:], 0.0).then_inc(pool_step, 1)
                pool.memset(xv_ones[:], 0.0).then_inc(pool_step, 1)
                pool.wait_ge(pool_step, 2)
                pool.memset(v_ones[:, :, :, DH:DH + 1], 1.0).then_inc(pool_step, 1)
                pool.wait_ge(pool_step, 3)
                pool.memset(xv_ones[0:M, :, DH:DH + 1], 1.0).then_inc(pool_step, 1)
                pool.wait_ge(pool_step, 4)
                pool.memset(xv_ones[M:P, :, VW + DH:VW + DH + 1], 1.0).then_inc(pool_step, 1)

            @block.vector
            def _(dve):
                count = [0]

                def link(ins):
                    count[0] += 1
                    ins.then_inc(prep_step, 1)
                    dve.wait_ge(prep_step, count[0])

                link(dve.memset(q_stack[:].bitcast(F32), 0.0))
                link(dve.memset(k_stack[:].bitcast(F32), 0.0))
                dve.memset(xmax[:].bitcast(F32), 0.0)
                dve.memset(q_stack[ONES_ROW:ONES_ROW + 2, :, :].bitcast(F32), 1.0)
                dve.memset(k_stack[MAX_ROW:MAX_ROW + 2, :, :].bitcast(F32), 1.0)
                dve.wait_ge(w_loaded, 16 * 16)
                dve.wait_ge(c_loaded, 16 * 9)
                dve.tensor_copy(eye_bf[:], eye[:])
                dve.tensor_copy(tri_bf[:], scratch[:, 0, 0:P])
                dve.tensor_copy(pick_max[:].rearrange("p a b -> p (a b)"),
                                o_tok[0:2 * 32, :, :].rearrange("p a b -> p (a b)"))\
                    .then_inc(alibi_used, 2)
                dve.wait_ge(lora_ready, 2 * 3)
                for j, n in enumerate(("q", "k", "v")):
                    for c in range(NC):
                        link(dve.scalar_tensor_tensor(
                            out=raw[n][:, c, :], in0=(scores + scores_t + outs)[2 * j + c][:, 0:D],
                            scalar=2.0, in1=raw[n][:, c, :], op0=ALU.mult, op1=ALU.add))
                link(dve.tensor_scalar(raw["q"], raw["q"], DH ** -0.5, None, ALU.mult))
                link(dve.tensor_scalar(raw["xq"], raw["xq"], DH ** -0.5, None, ALU.mult))
                dve.tensor_scalar(xq_bias[:], xq_bias[:], DH ** -0.5, None, ALU.mult)
                for n in names:
                    link(dve.tensor_copy(w_hi[n][:], raw[n]))
                    dve.tensor_tensor(w_lo[n][:], raw[n], w_hi[n][:].bitcast(F32), ALU.subtract)
                for part in range(H // 2):
                    dve.wait_ge(alibi_loaded[part % 2], 16 * (part // 2 + 1))
                    dve.tensor_copy(
                        k_stack[BIAS_ROW:BIAS_ROW + 2, 2 * part:2 * part + 2, :],
                        alibi[part % 2][BIAS_ROW:BIAS_ROW + 2, :, :].rearrange("r (h u) d -> r h (u d)", h=2))\
                        .then_inc(alibi_used, 1)

        pause, pool_pause = sem("pause"), sem("pool_pause")
        work_ready = Signal(sem("work_ready"), 8, 13, 13)
        work_hi = Signal(sem("work_hi"), 6, 6, 7)
        work_free = Signal(sem("work_free"), 8, 13, 13, first=2)
        scores_ready = Signal(sem("scores_ready"), 0, NQ * H, 2 * NQ)
        scores_read = Signal(sem("scores_read"), 0, NQ * H, 2 * NQ, first=2)
        scores_t_ready = Signal(sem("scores_t_ready"), 0, 3 * H, H // 2)
        exp_done = Signal(sem("exp_done"), 0, 3 * H, H // 2, first=2)
        probs_used = Signal(sem("probs_used"), 0, 3 * H, H // 2, first=NP_TILES)
        outs_read = Signal(sem("outs_read"), 0, NG, NG, first=2)
        x_in_loaded = Signal(sem("x_in_loaded"), 16)
        var_ready = Signal(sem("var_ready"), 1, 0, 1)
        rstd_ready = Signal(sem("rstd_ready"), 1, 0, 1)
        norm_ready = Signal(sem("norm_ready"), 1, 0, 1)
        qk_stored = Signal(sem("qk_stored"), 4 * 16)
        stack_loaded = [Signal(sem(f"stack_loaded{u}"), 6 * 16) for u in range(2)]
        max_loaded = [Signal(sem(f"max_loaded{u}"), 0, 2 * 16) for u in range(2)]
        v_ready = Signal(sem("v_ready"), 1)
        x_res_loaded = Signal(sem("x_res_loaded"), 16)
        ctx_loaded = Signal(sem("ctx_loaded"), 2 * 16)
        ctx_split = Signal(sem("ctx_split"), 0, 1)
        ctx_step = Signal(sem("ctx_step"), 0, 1)
        heads_ready = Signal(sem("heads_ready"), 0, 1)
        bias_added = Signal(sem("bias_added"), 0, 0, 1)
        eps_added = Signal(sem("eps_added"), 1, 0, 1)
        dve_step = Signal(sem("dve_step"), *DVE_STEPS)
        x2_stored = Signal(sem("x2_stored"), 0, 0, 2 * 16, first=1)

        xb = a["x"].rearrange("b (q p) d -> b p q d", p=P)
        x2b = x2_dram.rearrange("b (q p) d -> b p q d", p=P)

        def work_bank(sec, n):
            return work[(n + (13 if sec.name == "cross" else 0)) % 2]

        block = ctx.enter_context(nc.Block())

        @block.sync
        def _(sp):
            sp.sem_inc(x2_stored.sem, 1)

            def load_x_in(b):
                sp.dma_start(x_in[:], xb[b]).then_inc(x_in_loaded.sem, 16)

            def load_x_res(b):
                sp.dma_start(x_res[:], xb[b]).then_inc(x_res_loaded.sem, 16)

            def load_ctx(b):
                sp.dma_start(ctx_in[:, 0, :], a["ctx"][b, 0:P, :]).then_inc(ctx_loaded.sem, 16)
                sp.dma_start(ctx_in[0:DC - P, 1, :], a["ctx"][b, P:DC, :]).then_inc(ctx_loaded.sem, 16)

            def store_qk(sec):
                for n in range(4):
                    if n % 2 == 0:
                        sp.wait_ge(work_free.sem, sec(work_free, 4 + n))
                    sp.dma_start(stack_dram[n].rearrange("c h d t -> (h d) c t"), qk[n][:].bitcast(F32))\
                      .then_inc(qk_stored.sem, 16)

            def load_stacks(u):
                for r, (qn, kn) in enumerate(((0, 2), (1, 2), (0, 3))):
                    for stack, n in ((q_stack, qn), (k_stack, kn)):
                        sp.dma_start(stack[DH * r:DH * (r + 1), HC * u:HC * (u + 1), :].bitcast(F32),
                                     stack_dram[n, u].rearrange("h d t -> d h t"))\
                          .then_inc(stack_loaded[u].sem, 16)

            def store_max(sec, u):
                sp.wait_ge(work_free.sem, sec(work_free, (0, 4)[u] + 1))
                for r, rows in enumerate((max_hi, max_lo)):
                    sp.dma_start(q_stack[MAX_ROW + r:MAX_ROW + r + 1, HC * u:HC * (u + 1), :].bitcast(F32),
                                 rows[:].bitcast(F32))\
                      .then_inc(max_loaded[u].sem, 16)

            def batch(i, last, ahead):
                project, attend, cross = (Section(s, i, last) for s in ("project", "attend", "cross"))
                start = Section("start", i)
                if not last:
                    sp.wait_ge(stack_loaded[1].sem, start(stack_loaded[1], 0))
                    store_qk(project)
                store_max(attend, 0)
                if ahead:
                    sp.wait_ge(norm_ready.sem, project(norm_ready, 1))
                    load_x_in(i + 2)
                if not last:
                    sp.wait_ge(ctx_split.sem, attend(ctx_split, 1))
                    load_ctx(i + 1)
                store_max(attend, 1)
                if not last:
                    sp.wait_ge(qk_stored.sem, project(qk_stored, 64))
                    for u in range(2):
                        sp.wait_ge(scores_t_ready.sem, attend(scores_t_ready, 3 * HC * (u + 1)))
                        load_stacks(u)
                    sp.wait_ge(norm_ready.sem, cross(norm_ready, 1))
                    sp.wait_ge(bias_added.sem, cross(bias_added, 1))
                    load_x_res(i + 1)
                for u in range(2):
                    sp.wait_ge(work_free.sem, cross(work_free, 12 + u))
                    sp.dma_start(x2b[i, :, 2 * u:2 * u + 2, :], x_out[:, 2 * u:2 * u + 2, :])\
                      .then_inc(x2_stored.sem, 16)

            load_x_in(0)
            load_ctx(0)
            load_x_res(0)
            sec = Section("project")
            sp.wait_ge(norm_ready.sem, sec(norm_ready, 1))
            load_x_in(1)
            store_qk(sec)
            sp.wait_ge(qk_stored.sem, sec(qk_stored, 64))
            for u in range(2):
                load_stacks(u)
            with sp.Fori(0, B - 2) as i:
                batch(i, False, True)
            batch(B - 2, False, False)
            batch(B - 1, True, False)
            sp.wait_ge(x2_stored.sem, 1 + 32 * B)

        @block.gpsimd
        def _(pool):
            def rstd_of(sec):
                pool.wait_ge(var_ready.sem, sec(var_ready, 1))
                pool.sem_inc(pool_pause, 1)
                pool.tensor_scalar(rstd[:], mean_var[:, :, 1], EPS, None, ALU.add)\
                    .then_inc(eps_added.sem, 1)
                pool.wait_ge(eps_added.sem, sec(eps_added, 1))
                pool.tensor_tensor(rstd[:], rstd[:], power[:], ALU.pow).then_inc(rstd_ready.sem, 1)

            def batch(i, last):
                project, attend, cross = (Section(s, i, last) for s in ("project", "attend", "cross"))
                start = Section("start", i)
                pool.wait_ge(ctx_loaded.sem, start(ctx_loaded, 0))
                pool.sem_inc(pool_pause, 1)
                src = ctx_in[:].rearrange("p c (o m) -> p c o m", o=1).to_broadcast([P, 2, 2, M])
                dst = [t[:].rearrange("p c (o m) -> p c o m", o=2) for t in (ctx_hi, ctx_lo)]
                pool.tensor_copy(dst[0], src).then_inc(ctx_step.sem, 1)
                pool.wait_ge(ctx_step.sem, attend(ctx_step, 1))
                pool.tensor_tensor(dst[1], src, dst[0].bitcast(F32), ALU.subtract)\
                    .then_inc(ctx_split.sem, 1)
                if not last:
                    rstd_of(project)
                pool.wait_ge(work_free.sem, attend(work_free, 3))
                for half, heads in ((xk_hi, xk_hi_heads), (xk_lo, xk_lo_heads)):
                    for c in range(NC):
                        last_one = pool.tensor_tensor(
                            heads[:, c, :].rearrange("p (h m) -> p h m", h=HC),
                            half[:, c:c + 1, :].bitcast(F32).to_broadcast([P, HC, M]),
                            head_mask[:], ALU.mult)
                last_one.then_inc(heads_ready.sem, 1)
                rstd_of(cross)
                pool.wait_ge(work_free.sem, attend(work_free, 13))
                pool.wait_ge(x2_stored.sem, start(x2_stored, 0))
                pool.tensor_tensor(x_out[:], x_res[:],
                                   xo_bias[:].rearrange("p (o d) -> p o d", o=1).to_broadcast([P, NQ, D]),
                                   ALU.add).then_inc(bias_added.sem, 1)

            rstd_of(Section("project"))
            with pool.Fori(0, B - 1) as i:
                batch(i, False)
            batch(B - 1, True)

        @block.scalar
        def _(act):
            act.sem_inc(exp_done.sem, 2)
            act.sem_inc(outs_read.sem, 2)

            def hi_part(sec, n, dst, src, scale=1.0, bias=None):
                act.wait_ge(work_ready.sem, sec(work_ready, n + 1))
                if bias is not None:
                    ins = act.activation(dst, src, ACT.Identity, bias=bias, scale=1.0)
                elif scale != 1.0:
                    ins = act.mul(dst, src, scale)
                else:
                    ins = act.copy(dst, src)
                ins.then_inc(work_hi.sem, 1)

            def values(sec_v, sec_used, used):
                act.wait_ge(work_free.sem, sec_v(work_free, 8))
                if sec_used is not None:
                    act.wait_ge(probs_used.sem, sec_used(probs_used, used))
                act.copy(v_ones[:, :, :, 0:DH], v_next[:].rearrange("p q (h d) -> p q h d", d=DH))\
                   .then_inc(v_ready.sem, 1)

            def project_batch(sec):
                for c in range(NC):
                    hi_part(sec, c, feat_hi[:, c, :], work_bank(sec, c)[:])
                for n in range(4):
                    hi_part(sec, 2 + n, qk[2 * (n // 2)][:, n % 2, :], work_bank(sec, 2 + n)[:])

            def exp(sec, n, width):
                act.wait_ge(scores_t_ready.sem, sec(scores_t_ready, n + 1))
                act.wait_ge(probs_used.sem, sec(probs_used, n + 1 - NP_TILES))
                slot = (n + (3 * H if sec.name == "cross" else 0)) % NP_TILES
                act.activation(probs[slot][:, 0:width], scores_t[n % 2][:, 0:width], ACT.Exp)\
                   .then_inc(exp_done.sem, 1)

            def read_outs(sec, g, used):
                act.wait_ge(probs_used.sem, sec(probs_used, used))
                act.copy(o_ext[g % 2][:], outs[g % 2][:]).then_inc(outs_read.sem, 1)

            def back(sec):
                for c in range(NC):
                    hi_part(sec, 9 + c, feat_hi[:, c, :], work_bank(sec, 9 + c)[:])

            def batch(i, last):
                project, attend, cross = (Section(s, i, last) for s in ("project", "attend", "cross"))
                if not last:
                    project_batch(project)
                hi_part(attend, 0, max_hi[:], work_bank(attend, 0)[0:HC, :], scale=-1.0)
                for c in range(NC):
                    hi_part(attend, 1 + c, xk_hi[:, c, :], work_bank(attend, 1 + c)[:, 0:M],
                            bias=xk_bias[:, c:c + 1])
                for h in range(H):
                    if h == M1_STEP:
                        hi_part(attend, 4, max_hi[:], work_bank(attend, 4)[0:HC, :], scale=-1.0)
                    for k, width in enumerate((512, 512, 256)):
                        exp(attend, 3 * h + k, width)
                    if h % GH == 0 and h:
                        read_outs(attend, h // GH - 1, 3 * h)
                read_outs(attend, NG - 1, 3 * H)
                if not last:
                    values(project, attend, 3 * H)
                back(attend)
                for c in range(NC):
                    hi_part(cross, c, feat_hi[:, c, :], work_bank(cross, c)[:])
                if not last:
                    act.wait_ge(qk_stored.sem, project(qk_stored, 64))
                for c in range(NC):
                    hi_part(cross, 2 + c, qk[0][:, c, :], work_bank(cross, 2 + c)[:],
                            bias=xq_bias[:, c:c + 1])
                hi_part(cross, 4, xmax[0:H, :], work_bank(cross, 4)[0:H, :], scale=-1.0)
                for p in range(H // 2):
                    exp(cross, p, 512)
                    if p % 2 == 0 and p:
                        read_outs(cross, p // 2 - 1, p)
                read_outs(cross, NG - 1, H // 2)
                back(cross)

            project_batch(Section("project"))
            values(Section("project"), None, 0)
            with act.Fori(0, B - 1) as i:
                batch(i, False)
            batch(B - 1, True)

        @block.vector
        def _(dve):
            dve.sem_inc(work_free.sem, 2)
            dve.sem_inc(scores_read.sem, 2)
            steps = {"project": 0, "attend": 0, "cross": 0}

            def link(sec, ins):
                steps[sec.name] += 1
                ins.then_inc(dve_step.sem, 1)
                dve.wait_ge(dve_step.sem, sec(dve_step, steps[sec.name]))

            def layer_norm(sec, src):
                for q in range(NQ):
                    ins = dve.bn_stats(stats[:, q, :], src[:, q, :])
                link(sec, ins)
                dve.sem_inc(pause, 1)
                for q in range(NQ):
                    ins = dve.bn_aggr(mean_var[:, q, :], stats[:, q, :])
                ins.then_inc(var_ready.sem, 1)
                dve.wait_ge(rstd_ready.sem, sec(rstd_ready, 1))
                for q in range(NQ):
                    ins = dve.tensor_scalar(x_norm[:, q, :], src[:, q, :], mean_var[:, q, 0:1],
                                            rstd[:, q:q + 1], ALU.subtract, ALU.mult)
                ins.then_inc(norm_ready.sem, 1)

            def lo_part(sec, k, dst, src, hi, scale=1.0, bias=None):
                dve.wait_ge(work_hi.sem, sec(work_hi, k + 1))
                if bias is not None:
                    ins = dve.scalar_tensor_tensor(out=dst, in0=src, scalar=bias, in1=hi.bitcast(F32),
                                                   op0=ALU.add, op1=ALU.subtract)
                elif scale != 1.0:
                    ins = dve.scalar_tensor_tensor(out=dst, in0=src, scalar=scale, in1=hi.bitcast(F32),
                                                   op0=ALU.mult, op1=ALU.subtract)
                else:
                    ins = dve.tensor_tensor(dst, src, hi.bitcast(F32), ALU.subtract)
                ins.then_inc(work_free.sem, 1)

            def project_steps(sec, first):
                def feat(c):
                    return lambda: lo_part(sec, c, feat_lo[:, c, :], work_bank(sec, c)[:], feat_hi[:, c, :])

                def qk_lo(n):
                    w = 2 * (n // 2)
                    return lambda: lo_part(sec, 2 + n, qk[w + 1][:, n % 2, :], work_bank(sec, 2 + n)[:],
                                           qk[w][:, n % 2, :])

                def v_half(u):
                    def step():
                        if not first:
                            dve.wait_ge(v_ready.sem, Section("start", sec.i)(v_ready, 0))
                        dve.wait_ge(work_ready.sem, sec(work_ready, 7 + u))
                        dve.tensor_copy(v_next[:, 2 * u:2 * u + 2, :].rearrange("p q d -> p (q d)"),
                                        work_bank(sec, 6 + u)[:]).then_inc(work_free.sem, 1)
                    return step

                return [feat(0), feat(1)] + [qk_lo(n) for n in range(4)] + [v_half(u) for u in range(2)]

            def maxima(sec, h):
                for t in range(NQ):
                    n = NQ * h + t
                    w = P * (t + 1)
                    dve.wait_ge(scores_ready.sem, sec(scores_ready, n + 1))
                    dve.sem_inc(pause, 1)
                    dve.tensor_tensor_reduce(out=scratch[:, n % 2, 0:w], in0=scores[n % 2][:, 0:w],
                                             in1=row_mask[:, T - w:T], scale=1.0, scalar=LOWEST,
                                             op0=ALU.add, op1=ALU.max,
                                             accum_out=row_max[:, t, h:h + 1]).then_inc(scores_read.sem, 1)

            def normalise(sec, g):
                dve.wait_ge(work_ready.sem, sec(work_ready, 5 + g + 1))
                o = work_bank(sec, 5 + g)[:].rearrange("p (t j d) -> p t j d", t=NQ, j=GH)
                link(sec, dve.reciprocal(o_sum[:, g % 2], o[:, :, :, DH]))
                dve.tensor_tensor(
                    o_tok[:].rearrange("p t (g j d) -> p g t j d", g=NG, j=GH)[:, g],
                    o[:, :, :, 0:DH],
                    o_sum[:, g % 2].rearrange("p t (j o) -> p t j o", o=1).to_broadcast([P, NQ, GH, DH]),
                    ALU.mult).then_inc(work_free.sem, 1)

            def back(sec, k):
                for c in range(NC):
                    lo_part(sec, k + c, feat_lo[:, c, :], work_bank(sec, 9 + c)[:], feat_hi[:, c, :])

            def batch(i, last):
                project, attend, cross = (Section(s, i, last) for s in ("project", "attend", "cross"))
                start = Section("start", i)
                side = []
                if not last:
                    steps["project"] = 0
                    dve.wait_ge(x_in_loaded.sem, project(x_in_loaded, 16))
                    layer_norm(project, x_in)
                    side = project_steps(project, False)
                for h in range(HC):
                    maxima(attend, h)
                    if h and side:
                        side.pop(0)()
                        if h == 1:
                            side.pop(0)()
                for step in side:
                    step()
                lo_part(attend, 0, max_lo[:], work_bank(attend, 0)[0:HC, :], max_hi[:], scale=-1.0)
                for c in range(NC):
                    lo_part(attend, 1 + c, xk_lo[:, c, :], work_bank(attend, 1 + c)[:, 0:M],
                            xk_hi[:, c, :], bias=xk_bias[:, c:c + 1])
                dve.wait_ge(work_ready.sem, attend(work_ready, 4))
                v = work_bank(attend, 3)[:, 0:D].rearrange("p (a o d) -> p a o d", o=2, d=DH)
                vb = xv_bias[:].rearrange("p (a o d) -> p a o d", o=2, d=DH)
                dve.tensor_tensor(xv_ones[0:M, :, 0:DH], v[0:M, :, 0, :], vb[0:M, :, 0, :], ALU.add)
                dve.tensor_tensor(xv_ones[M:P, :, VW:VW + DH], v[M:P, :, 1, :], vb[M:P, :, 1, :],
                                  ALU.add).then_inc(work_free.sem, 1)
                for step in range(H + 2):
                    for h in PASS1_AT.get(step, ()):
                        maxima(attend, h)
                    if step == M1_STEP:
                        lo_part(attend, 3, max_lo[:], work_bank(attend, 4)[0:HC, :], max_hi[:], scale=-1.0)
                    if step % GH == 1 and step > 1:
                        normalise(attend, step // GH - 1)
                back(attend, 4)
                dve.wait_ge(x_res_loaded.sem, start(x_res_loaded, 0))
                for u in range(2):
                    dve.wait_ge(work_ready.sem, attend(work_ready, 12 + u))
                    r = x_res[:, 2 * u:2 * u + 2, :].rearrange("p q d -> p (q d)")
                    dve.tensor_tensor(r, work_bank(attend, 11 + u)[:], r, ALU.add)\
                       .then_inc(work_free.sem, 1)
                dve.wait_ge(work_free.sem, attend(work_free, 13))
                layer_norm(cross, x_res)
                for c in range(NC):
                    lo_part(cross, c, feat_lo[:, c, :], work_bank(cross, c)[:], feat_hi[:, c, :])
                for c in range(NC):
                    lo_part(cross, 2 + c, qk[1][:, c, :], work_bank(cross, 2 + c)[:], qk[0][:, c, :],
                            bias=xq_bias[:, c:c + 1])
                for n in range(2 * NQ):
                    dve.wait_ge(scores_ready.sem, cross(scores_ready, n + 1))
                    dve.tensor_reduce(row_max[:, n // 2, HC * (n % 2):HC * (n % 2 + 1)],
                                      scores[n % 2][:].rearrange("p (h m) -> p h m", h=HC),
                                      AX.X, ALU.max).then_inc(scores_read.sem, 1)
                lo_part(cross, 4, xmax[32:32 + H, :], work_bank(cross, 4)[0:H, :], xmax[0:H, :], scale=-1.0)
                for g in range(NG):
                    normalise(cross, g)
                back(cross, 5)
                dve.wait_ge(bias_added.sem, cross(bias_added, 1))
                for u in range(2):
                    dve.wait_ge(work_ready.sem, cross(work_ready, 12 + u))
                    r = x_out[:, 2 * u:2 * u + 2, :].rearrange("p q d -> p (q d)")
                    dve.tensor_tensor(r, work_bank(cross, 11 + u)[:], r, ALU.add)\
                       .then_inc(work_free.sem, 1)
                steps.update(attend=0, cross=0)

            sec = Section("project")
            dve.wait_ge(x_in_loaded.sem, sec(x_in_loaded, 16))
            layer_norm(sec, x_in)
            for step in project_steps(sec, True):
                step()
            with dve.Fori(0, B - 1) as i:
                batch(i, False)
            batch(B - 1, True)

        @block.tensor
        def _(pe):
            pe.sem_inc(probs_used.sem, NP_TILES)

            def fill(sec, n):
                pe.wait_ge(work_free.sem, sec(work_free, n - 1))
                return work_bank(sec, n)

            def passes(out, pairs, start=True, stop=True):
                todo = [(w, x) for (wh, wl), (xh, xl) in pairs for w, x in ((wh, xh), (wl, xh), (wh, xl))]
                for j, (w, x) in enumerate(todo):
                    ins = pe.matmul(out, w, x, start=start and j == 0, stop=stop and j == len(todo) - 1)
                return ins

            def turn(sec, n, out_rows, src):
                out = fill(sec, n)
                for t in range(NQ):
                    ins = pe.transpose(out[0:out_rows, t * P:(t + 1) * P], src(t), eye[:])
                ins.then_inc(work_ready.sem, 1)

            def feat(c, s=slice(None)):
                return feat_hi[:, c, s], feat_lo[:, c, s]

            def weight(n, c, s=slice(None)):
                return w_hi[n][:, c, s], w_lo[n][:, c, s]

            def by_features(sec, n, w, m):
                out = fill(sec, n)
                passes(out[:], [(weight(w, c, slice(m * P, (m + 1) * P)), feat(c)) for c in range(NC)])\
                    .then_inc(work_ready.sem, 1)

            def by_tokens(sec, n, w, u):
                out = fill(sec, n)
                for t in (2 * u, 2 * u + 1):
                    ins = passes(out[:, D * (t % 2):D * (t % 2 + 1)],
                                 [(feat(c, slice(t * P, (t + 1) * P)), weight(w, c)) for c in range(NC)])
                ins.then_inc(work_ready.sem, 1)

            def norm_turn(sec):
                pe.wait_ge(norm_ready.sem, sec(norm_ready, 1))
                for c in range(NC):
                    turn(sec, c, P, lambda t: x_norm[:, t, c * P:(c + 1) * P])

            def project_steps(sec):
                def q_or_k(n):
                    def step():
                        if n == 0:
                            pe.wait_ge(work_free.sem, sec(work_free, 2))
                        by_features(sec, 2 + n, "qk"[n // 2], n % 2)
                    return step
                return [lambda: norm_turn(sec)] + [q_or_k(n) for n in range(4)] \
                    + [(lambda u: lambda: by_tokens(sec, 6 + u, "v", u))(u) for u in range(2)]

            def rows(sec, h):
                for t in range(NQ):
                    n = NQ * h + t
                    pe.wait_ge(scores_read.sem, sec(scores_read, n - 1))
                    pe.matmul(scores[n % 2][:, 0:P * (t + 1)], q_stack[0:MAX_ROW, h, t * P:(t + 1) * P],
                              k_stack[0:MAX_ROW, h, 0:P * (t + 1)], start=True, stop=True)\
                      .then_inc(scores_ready.sem, 1)

            def turn_maxima(sec, n, done, lo, hi):
                pe.wait_ge(scores_read.sem, sec(scores_read, done))
                turn(sec, n, hi - lo, lambda t: row_max[:, t, lo:hi])

            def columns(sec, h, k):
                n = 3 * h + k
                pe.wait_ge(exp_done.sem, sec(exp_done, n - 1))
                bank = scores_t[n % 2]
                for kt, col, w in PARTS[k]:
                    pe.matmul(bank[:, col:col + w], k_stack[0:MAX_ROW + 2, h, kt * P:(kt + 1) * P],
                              q_stack[0:MAX_ROW + 2, h, kt * P:T], start=True, stop=False)
                    ins = pe.matmul(bank[:, col:col + P], eye_bf[:], tri_bf[:], start=False, stop=True)
                ins.then_inc(scores_t_ready.sem, 1)

            def weigh(sec, h, k):
                n = 3 * h + k
                pe.wait_ge(exp_done.sem, sec(exp_done, n + 1))
                g, j = h // GH, h % GH
                if j == 0 and k == 0:
                    pe.wait_ge(outs_read.sem, sec(outs_read, g - 1))
                for kt, col, w in PARTS[k]:
                    ins = pe.matmul(outs[g % 2][VW * j:VW * (j + 1), kt * P:T], v_ones[:, kt, h, :],
                                    probs[n % NP_TILES][:, col:col + w], start=(k == 0), stop=(kt == 2),
                                    tile_position=(0, VW * j))
                ins.then_inc(probs_used.sem, 1)

            def turn_outs(sec, g):
                pe.wait_ge(outs_read.sem, sec(outs_read, g + 1))
                turn(sec, 5 + g, P, lambda t: o_ext[g % 2][:, t * P:(t + 1) * P])

            def finish(sec, w):
                pe.wait_ge(work_free.sem, sec(work_free, 9))
                for c in range(NC):
                    turn(sec, 9 + c, P, lambda t: o_tok[:, t, c * P:(c + 1) * P])
                pe.wait_ge(work_free.sem, sec(work_free, 11))
                for u in range(2):
                    by_tokens(sec, 11 + u, w, u)

            def batch(i, last):
                project, attend, cross = (Section(s, i, last) for s in ("project", "attend", "cross"))
                start = Section("start", i)
                side = [] if last else project_steps(project)
                pe.wait_ge(stack_loaded[0].sem, start(stack_loaded[0], 0))
                for h in range(HC):
                    rows(attend, h)
                    if h and side:
                        side.pop(0)()
                for step in side:
                    step()
                turn_maxima(attend, 0, NQ * HC, 0, HC)
                pe.wait_ge(ctx_split.sem, attend(ctx_split, 1))
                for m in range(NC):
                    out = fill(attend, 1 + m)
                    passes(out[:, 0:M], [(weight("xk", c, slice(m * P, (m + 1) * P)),
                                          (ctx_hi[:, c, 0:M], ctx_lo[:, c, 0:M])) for c in range(2)])\
                        .then_inc(work_ready.sem, 1)
                out = fill(attend, 3)
                passes(out[:, 0:D], [((ctx_hi[:, c, :], ctx_lo[:, c, :]), weight("xv", c))
                                     for c in range(2)]).then_inc(work_ready.sem, 1)
                pe.wait_ge(stack_loaded[1].sem, start(stack_loaded[1], 0))
                for step in range(H + 2):
                    for h in PASS1_AT.get(step, ()):
                        rows(attend, h)
                    if step == M1_STEP:
                        turn_maxima(attend, 4, NQ * H, HC, H)
                    if step % HC == 0 and step < H:
                        pe.wait_ge(max_loaded[step // HC].sem, attend(max_loaded[step // HC], 32))
                    if step == 1:
                        pe.wait_ge(v_ready.sem, start(v_ready, 0))
                    for k in range(3):
                        if step < H:
                            columns(attend, step, k)
                        if 1 <= step <= H:
                            weigh(attend, step - 1, k)
                    if step % GH == 1 and step > 1:
                        turn_outs(attend, step // GH - 1)
                finish(attend, "p")

                norm_turn(cross)
                pe.wait_ge(work_free.sem, cross(work_free, 2))
                for m in range(NC):
                    by_features(cross, 2 + m, "xq", m)
                pe.wait_ge(work_free.sem, cross(work_free, 4))
                pe.wait_ge(heads_ready.sem, attend(heads_ready, 1))
                for n in range(2 * NQ):
                    t, c = n // 2, n % 2
                    pe.wait_ge(scores_read.sem, cross(scores_read, n - 1))
                    pe.matmul(scores[n % 2][:], qk[0][:, c, t * P:(t + 1) * P], xk_hi_heads[:, c, :],
                              start=True, stop=True).then_inc(scores_ready.sem, 1)
                turn_maxima(cross, 4, 2 * NQ, 0, H)
                pe.wait_ge(work_free.sem, cross(work_free, 5))
                for p in range(H // 2 + 1):
                    if p < H // 2:
                        pe.wait_ge(exp_done.sem, cross(exp_done, p - 1))
                        c, s = p // GH, slice((p % GH) * P, (p % GH + 1) * P)
                        passes(scores_t[p % 2][:], [((xk_hi_heads[:, c, s], xk_lo_heads[:, c, s]),
                                                     (qk[0][:, c, :], qk[1][:, c, :]))], stop=False)
                        pe.matmul(scores_t[p % 2][:], pick_max[:, p, :], xmax[:], start=False, stop=True)\
                          .then_inc(scores_t_ready.sem, 1)
                    if p:
                        n, g = p - 1, (p - 1) // 2
                        pe.wait_ge(exp_done.sem, cross(exp_done, n + 1))
                        if n % 2 == 0:
                            pe.wait_ge(outs_read.sem, cross(outs_read, g - 1))
                        base = 2 * VW * (n % 2)
                        pe.matmul(outs[g % 2][base:base + 2 * VW, :], xv_ones[:, n, :],
                                  probs[(3 * H + n) % NP_TILES][:], start=True, stop=True,
                                  tile_position=(0, base)).then_inc(probs_used.sem, 1)
                    if p >= 4 and p % 2 == 0:
                        turn_outs(cross, p // 2 - 2)
                turn_outs(cross, NG - 1)
                finish(cross, "xo")

            for step in project_steps(Section("project")):
                step()
            with pe.Fori(0, B - 1) as i:
                batch(i, False)
            batch(B - 1, True)


UNROLL = 4
ROW = D + 2
TOKENS = B * T
PAIRS = 2 * TOKENS
REGION = TOKENS + P
SLOT_TILES = -(-(PAIRS // P + E - 1) // UNROLL) * UNROLL
PAD_TILES = SLOT_TILES - PAIRS // P
RQ = 8
assert PAD_TILES == E == RQ
RG = TOKENS // (RQ * P)


class Flow:

    def __init__(self, sem, first=0, per=1):
        self.sem, self.first, self.per = sem, first, per

    def at(self, u, n):
        return self.per * u + (self.first + self.per * n)


def run_pipeline(engine, units, stages):
    for s in range(2 * UNROLL):
        for lag, stage in stages:
            if s >= lag:
                stage(s - lag, (s - lag) % UNROLL)
    with engine.Fori(2, units // UNROLL) as i:
        for s in range(UNROLL):
            for lag, stage in stages:
                stage(UNROLL * i + (s - lag), (s - lag) % UNROLL)
    for s in range(max(lag for lag, _ in stages)):
        for lag, stage in stages:
            if s < lag:
                stage(units + s - lag, (s - lag) % UNROLL)


def mixture(nc, a, x2_dram, out):
    ctx = ExitStack()
    with ctx:
        def sb(name, shape, dt=F32, into=ctx):
            return into.enter_context(nc.sbuf_tensor(name, shape, dt))

        up_hi = sb("up_hi", [P, NE, NC, 2 * HID], F32R)
        up_lo = sb("up_lo", [P, NE, NC, 2 * HID], F32R)
        down_hi = sb("down_hi", [P, NE, HID // P, D], F32R)
        down_lo = sb("down_lo", [P, NE, HID // P, D], F32R)
        eye = sb("f_eye", [P, P])
        where = sb("where", [P, 2, SLOT_TILES], U32)
        regions = nc.dram_tensor("regions", (E * REGION + PAD_TILES * P, ROW), F32, kind="Internal").ap()
        shares = nc.dram_tensor("shares", (PAIRS + 2 * PAD_TILES * P, D), F32, kind="Internal").ap()
        weights = (up_hi, up_lo, down_hi, down_lo)
        route(nc, a, x2_dram, weights, eye, where, regions)
        swiglu(nc, weights, eye, where=where, regions=regions, shares=shares)
        swiglu(nc, weights, eye, x2_dram=x2_dram, shares=shares, out=out)


def route(nc, a, x2_dram, weights, eye, where, regions):
    up_hi, up_lo, down_hi, down_lo = weights
    ctx = ExitStack()
    with ctx:
        def sb(name, shape, dt=F32):
            return ctx.enter_context(nc.sbuf_tensor(name, shape, dt))

        def bank(name):
            return ctx.enter_context(nc.psum_tensor(name, [P, 512], F32))

        def sem(name):
            return ctx.enter_context(nc.semaphore(name))

        router = sb("router", [P, NC, E])
        expert_bias = sb("expert_bias", [P, E])
        expert_no = sb("expert_no", [P, E])
        region_start = sb("region_start", [P, E + 1])
        before = sb("before", [P, P])
        before_bf = sb("before_bf", [P, P], BF16)
        ones_bf = sb("ones_bf", [P, P], BF16)
        up_to = sb("up_to", [P, E, E])
        tile_no = sb("tile_no", [P, SLOT_TILES])
        tile_start = sb("tile_start", [P, TOKENS // P])
        pad_dest = sb("pad_dest", [P, 2, RQ])
        part_no = sb("part_no", [P, 1])
        power = sb("f_power", [P, RQ])
        raw_up = sb("raw_up", [P, NC, 2 * HID])
        raw_down = sb("raw_down", [P, HID // P, D])

        x_in = sb("f_x_in", [P, RQ, D])
        stats = sb("f_stats", [P, RQ, 6])
        mean_var = sb("f_mean_var", [P, RQ, 2])
        rstd = sb("f_rstd", [P, RQ])
        rows = [sb(f"rows{n}", [P, 2, RQ, ROW]) for n in range(2)]
        dest = [sb(f"dest{n}", [P, 2, RQ]) for n in range(2)]
        feat = sb("f_feat", [P, NC, RQ * P])
        logits = sb("logits", [P, RQ, E])
        top_logit = sb("top_logit", [P, RQ])
        weight_sum = sb("weight_sum", [P, RQ])
        weight = sb("weight", [P, RQ, E])
        biased = sb("biased", [P, RQ, E])
        top = sb("top", [P, RQ, 8])
        top_at = sb("top_at", [P, RQ, 8], U32)
        top_no = sb("top_no", [P, RQ, 8])
        chosen = sb("chosen", [P, 2, RQ, E])
        chosen_bf = sb("chosen_bf", [P, RQ, E], BF16)
        picked = sb("picked", [P, 2, RQ, E])
        place = sb("place", [P, RQ, E])
        picked_place = sb("picked_place", [P, 2, RQ, E])
        slot = sb("slot", [P, 2, RQ])
        slot_no = [sb(f"slot_no{n}", [P, 2 * RQ], U32) for n in range(2)]
        next_row = [sb(f"next_row{n}", [P, E]) for n in range(2)]
        pad_row = sb("pad_row", [P, E])
        pad_no = sb("pad_no", [P, E], U32)
        filled = sb("filled", [P, E, TOKENS // P])
        tiles = sb("tiles", [P, E])
        upto_tiles = sb("upto_tiles", [P, E, E])
        end_tile = sb("end_tile", [P, E])
        first = sb("first", [P, E + 1])
        jump = sb("jump", [P, E])
        passed = sb("passed", [P, SLOT_TILES, E])
        jumped = sb("jumped", [P, SLOT_TILES, E])
        tile_expert = sb("tile_expert", [P, SLOT_TILES])
        tile_row = sb("tile_row", [P, SLOT_TILES])

        turned = [bank(f"r_turned{n}") for n in range(4)]
        logit_bank = bank("logit_bank")
        rank_bank = bank("rank_bank")

        w_loaded = sem("f_w_loaded")
        w_hi_done = sem("f_w_hi_done")
        w_lo_done = sem("f_w_lo_done")
        c_loaded = sem("f_c_loaded")
        consts_ready = sem("consts_ready")
        prep_step = sem("f_prep_step")
        tail_step = sem("tail_step")
        pads_ready = sem("pads_ready")
        pads_stored = sem("pads_stored")
        pool_pause, pause = sem("f_pool_pause"), sem("f_pause")
        x_in_loaded = Flow(sem("f_x_in_loaded"), per=16)
        var_ready = Flow(sem("f_var_ready"))
        eps_added = Flow(sem("f_eps_added"))
        rstd_ready = Flow(sem("f_rstd_ready"))
        norm_ready = Flow(sem("f_norm_ready"))
        rows_copied = Flow(sem("rows_copied"))
        turned_ready = Flow(sem("r_turned_ready"))
        feat_ready = Flow(sem("r_feat_ready"))
        logits_ready = Flow(sem("logits_ready"))
        logits_read = Flow(sem("logits_read"))
        weighed = Flow(sem("weighed"))
        chosen_ready = Flow(sem("chosen_ready"))
        ranks_ready = Flow(sem("ranks_ready"))
        slots_ready = Flow(sem("slots_ready"))
        scattered = [Flow(sem(f"scattered{n}"), per=2 * RQ * 16) for n in range(2)]
        dve_step = Flow(sem("f_dve_step"), per=16)

        xg = x2_dram.rearrange("b t d -> (b t) d").rearrange("(g q p) d -> g p q d", p=P, q=RQ)

        block = ctx.enter_context(nc.Block())

        @block.sync
        def _(sp):
            sp.dma_start(x_in[:], xg[0]).then_inc(x_in_loaded.sem, 16)
            consts = ((eye[:], a["eye"]), (router[:], a["router_w"].rearrange("(c p) e -> p c e", p=P)),
                      (expert_bias[:], a["expert_bias"]), (expert_no[:], a["expert_no"]),
                      (region_start[:], a["region_start"]), (before[:], a["before"]),
                      (up_to[:], a["up_to"]), (tile_no[:], a["tile_no"]), (tile_start[:], a["tile_start"]),
                      (dest[0][:], a["dest"]), (pad_dest[:], a["pad_dest"]), (part_no[:], a["part_no"]))
            assert len(consts) == 12
            for dst, src in consts:
                sp.dma_start(dst, src).then_inc(c_loaded, 16)

            def load_weights(e):
                if e:
                    sp.wait_ge(w_lo_done, e)
                sp.dma_start(raw_up[:], a["w_up"][e].rearrange("(c p) n -> p c n", p=P))\
                  .then_inc(w_loaded, 16)
                sp.dma_start(raw_down[:], a["w_down"][e].rearrange("(c p) n -> p c n", p=P))\
                  .then_inc(w_loaded, 16)

            load_weights(0)
            load_weights(1)
            for g in range(1, RG):
                sp.wait_ge(norm_ready.sem, norm_ready.at(g, 0))
                sp.dma_start(x_in[:], xg[g]).then_inc(x_in_loaded.sem, 16)
                load_weights(g + 1)
            sp.wait_ge(pads_ready, 1)
            sp.dma_start(regions[E * REGION:, :].rearrange("(n p) d -> p n d", p=P), rows[0][:, 1])\
              .then_inc(pads_stored, 16)
            sp.wait_ge(pads_stored, 16)

        @block.gpsimd
        def _(pool):
            pool.memset(power[:], -0.5)
            pool.memset(ones_bf[:], 1.0).then_inc(consts_ready, 1)

            def split(e):
                pool.wait_ge(w_hi_done, e + 1)
                pool.tensor_tensor(up_lo[:, e], raw_up[:], up_hi[:, e].bitcast(F32), ALU.subtract)
                pool.tensor_tensor(down_lo[:, e], raw_down[:], down_hi[:, e].bitcast(F32),
                                   ALU.subtract).then_inc(w_lo_done, 1)

            split(0)
            for g in range(RG):
                pool.wait_ge(var_ready.sem, var_ready.at(g, 1))
                pool.tensor_scalar(rstd[:], mean_var[:, :, 1], EPS, None, ALU.add)\
                    .then_inc(eps_added.sem, 1)
                pool.wait_ge(eps_added.sem, eps_added.at(g, 1))
                pool.tensor_tensor(rstd[:], rstd[:], power[:], ALU.pow).then_inc(rstd_ready.sem, 1)
                split(g + 1)
                pool.wait_ge(rows_copied.sem, rows_copied.at(g, 1))
                pool.wait_ge(slots_ready.sem, slots_ready.at(g, 1))
                for j in range(2 * RQ):
                    pool.indirect_dma_start(
                        regions, bass.IndirectOffsetOnAxis(slot_no[g % 2][:, j:j + 1], 0),
                        rows[g % 2][:, j // RQ, j % RQ, :], None).then_inc(scattered[g % 2].sem, 16)
            pool.wait_ge(pads_ready, 1)
            for e in range(E):
                pool.indirect_dma_start(regions, bass.IndirectOffsetOnAxis(pad_no[:, e:e + 1], 0),
                                        rows[0][:, 0, e, :], None).then_inc(scattered[0].sem, 16)
            pool.wait_ge(scattered[0].sem, scattered[0].at(RG // 2, 0) + 16 * E)
            pool.wait_ge(scattered[1].sem, scattered[1].at(RG // 2, 0))

        @block.scalar
        def _(act):
            def split(e):
                act.wait_ge(w_loaded, 32 * (e + 1))
                act.copy(up_hi[:, e], raw_up[:])
                act.copy(down_hi[:, e], raw_down[:]).then_inc(w_hi_done, 1)

            split(0)
            for g in range(RG):
                act.wait_ge(norm_ready.sem, norm_ready.at(g, 1))
                act.copy(rows[g % 2][:, 1, :, 0:D], rows[g % 2][:, 0, :, 0:D]).then_inc(rows_copied.sem, 1)
                for c in range(NC):
                    for u in range(2):
                        act.wait_ge(turned_ready.sem, 4 * g + 2 * c + u + 1)
                        act.copy(feat[:, c, 512 * u:512 * (u + 1)], turned[2 * c + u][:])\
                           .then_inc(feat_ready.sem, 1)
                act.wait_ge(logits_read.sem, logits_read.at(g, 1))
                act.activation(weight[:], logits[:], ACT.Exp).then_inc(weighed.sem, 1)
                split(g + 1)

        @block.vector
        def _(dve):
            dve.wait_ge(c_loaded, 16 * 12)
            dve.tensor_copy(before_bf[:], before[:]).then_inc(consts_ready, 1)
            dve.tensor_copy(next_row[0][:], region_start[:, 0:E])
            for g in range(RG):
                steps = [0]
                s = g % 2

                def link(ins):
                    steps[0] += 1
                    ins.then_inc(dve_step.sem, 1)
                    dve.wait_ge(dve_step.sem, dve_step.at(g, 0) + steps[0])

                def spread(t):
                    return t.rearrange("p (q o) -> p q o", o=1).to_broadcast([P, RQ, E])

                dve.wait_ge(x_in_loaded.sem, x_in_loaded.at(g, 1))
                for q in range(RQ):
                    ins = dve.bn_stats(stats[:, q, :], x_in[:, q, :])
                link(ins)
                for q in range(RQ):
                    ins = dve.bn_aggr(mean_var[:, q, :], stats[:, q, :])
                ins.then_inc(var_ready.sem, 1)
                dve.wait_ge(rstd_ready.sem, rstd_ready.at(g, 1))
                if g >= 2:
                    dve.wait_ge(scattered[s].sem, scattered[s].at(g // 2, 0))
                for q in range(RQ):
                    ins = dve.tensor_scalar(rows[s][:, 0, q, 0:D], x_in[:, q, :], mean_var[:, q, 0:1],
                                            rstd[:, q:q + 1], ALU.subtract, ALU.mult)
                ins.then_inc(norm_ready.sem, 1)
                dve.tensor_copy(rows[s][:, :, :, D + 1], dest[s][:])
                dve.tensor_scalar(dest[1 - s][:], dest[s][:], float(RQ * P), None, ALU.add)
                dve.wait_ge(logits_ready.sem, logits_ready.at(g, 1))
                lg = logit_bank[:, 0:RQ * E].rearrange("p (q e) -> p q e", e=E)
                link(dve.tensor_reduce(top_logit[:], lg, AX.X, ALU.max))
                dve.tensor_tensor(logits[:], lg, spread(top_logit[:]), ALU.subtract)\
                    .then_inc(logits_read.sem, 1)
                dve.wait_ge(weighed.sem, weighed.at(g, 1))
                link(dve.tensor_reduce(weight_sum[:], weight[:], AX.X, ALU.add))
                link(dve.reciprocal(weight_sum[:], weight_sum[:]))
                link(dve.tensor_tensor(weight[:], weight[:], spread(weight_sum[:]), ALU.mult))
                link(dve.tensor_tensor(
                    biased[:], weight[:],
                    expert_bias[:].rearrange("p (o e) -> p o e", o=1).to_broadcast([P, RQ, E]), ALU.add))
                for q in range(RQ):
                    ins = dve.max(top[:, q, :], biased[:, q, :])
                link(ins)
                for q in range(RQ):
                    ins = dve.max_index(top_at[:, q, :], top[:, q, :], biased[:, q, :])
                link(ins)
                link(dve.tensor_copy(top_no[:], top_at[:]))
                for k in range(2):
                    ins = dve.tensor_tensor(
                        chosen[:, k], expert_no[:].rearrange("p (o e) -> p o e", o=1).to_broadcast([P, RQ, E]),
                        top_no[:, :, k:k + 1].to_broadcast([P, RQ, E]), ALU.is_equal)
                link(ins)
                dve.tensor_tensor(chosen_bf[:], chosen[:, 0], chosen[:, 1], ALU.add)\
                    .then_inc(chosen_ready.sem, 1)
                for k in range(2):
                    ins = dve.scalar_tensor_tensor(out=picked[:, k], in0=chosen[:, k], scalar=0.5,
                                                   in1=weight[:], op0=ALU.mult, op1=ALU.mult)
                link(ins)
                link(dve.tensor_reduce(rows[s][:, :, :, D], picked[:], AX.X, ALU.add))
                dve.wait_ge(ranks_ready.sem, ranks_ready.at(g, 1))
                rank = rank_bank[:, 0:RQ * E].rearrange("p (q e) -> p q e", e=E)
                dve.tensor_tensor(next_row[1 - s][:], rank_bank[:, RQ * E:(RQ + 1) * E], next_row[s][:], ALU.add)
                link(dve.tensor_tensor(
                    place[:], rank, next_row[s][:].rearrange("p (o e) -> p o e", o=1).to_broadcast([P, RQ, E]),
                    ALU.add))
                for k in range(2):
                    ins = dve.tensor_tensor(picked_place[:, k], chosen[:, k], place[:], ALU.mult)
                link(ins)
                link(dve.tensor_reduce(slot[:], picked_place[:], AX.X, ALU.add))
                link(dve.tensor_copy(slot_no[s][:], slot[:].rearrange("p k q -> p (k q)")))
                dve.sem_inc(slots_ready.sem, 1)
                assert steps[0] == dve_step.per, steps

            count = [0]

            def step(ins):
                count[0] += 1
                ins.then_inc(tail_step, 1)
                dve.wait_ge(tail_step, count[0])

            free = next_row[RG % 2]
            dve.tensor_scalar(pad_row[:], free[:], part_no[:, 0:1], None, ALU.add)
            dve.wait_ge(scattered[0].sem, scattered[0].at(RG // 2, 0))
            step(dve.memset(rows[0][:].rearrange("p k q d -> p (k q d)"), 0.0))
            dve.tensor_copy(rows[0][:, :, :, D + 1], pad_dest[:])
            step(dve.tensor_copy(pad_no[:], pad_row[:]))
            dve.sem_inc(pads_ready, 1)
            step(dve.tensor_tensor(tiles[:], free[:], region_start[:, 0:E], ALU.subtract))
            step(dve.tensor_tensor(
                filled[:], tile_start[:].rearrange("p (o j) -> p o j", o=1).to_broadcast([P, E, TOKENS // P]),
                tiles[:].rearrange("p (e o) -> p e o", o=1).to_broadcast([P, E, TOKENS // P]), ALU.is_lt))
            step(dve.tensor_reduce(tiles[:], filled[:], AX.X, ALU.add))
            step(dve.tensor_tensor(
                upto_tiles[:], up_to[:],
                tiles[:].rearrange("p (o e) -> p o e", o=1).to_broadcast([P, E, E]), ALU.mult))
            step(dve.tensor_reduce(end_tile[:], upto_tiles[:], AX.X, ALU.add))
            step(dve.memset(first[:], 0.0))
            step(dve.tensor_scalar(first[:, 1:E + 1], end_tile[:], -float(P), None, ALU.mult))
            step(dve.tensor_tensor(first[:], first[:], region_start[:], ALU.add))
            dve.tensor_tensor(jump[:], first[:, 1:E + 1], first[:, 0:E], ALU.subtract)
            step(dve.tensor_tensor(
                passed[:], end_tile[:].rearrange("p (o e) -> p o e", o=1).to_broadcast([P, SLOT_TILES, E]),
                tile_no[:].rearrange("p (j o) -> p j o", o=1).to_broadcast([P, SLOT_TILES, E]), ALU.is_le))
            dve.tensor_reduce(tile_expert[:], passed[:], AX.X, ALU.add)
            step(dve.tensor_tensor(
                jumped[:], passed[:],
                jump[:].rearrange("p (o e) -> p o e", o=1).to_broadcast([P, SLOT_TILES, E]), ALU.mult))
            step(dve.tensor_reduce(tile_row[:], jumped[:], AX.X, ALU.add))
            step(dve.scalar_tensor_tensor(out=tile_row[:], in0=tile_no[:], scalar=float(P), in1=tile_row[:],
                                          op0=ALU.mult, op1=ALU.add))
            step(dve.tensor_scalar(tile_expert[:], tile_expert[:], float(E - 1), None, ALU.min))
            dve.tensor_copy(where[:, 0, :], tile_row[:])
            step(dve.tensor_copy(where[:, 1, :], tile_expert[:]))

        @block.tensor
        def _(pe):
            pe.wait_ge(c_loaded, 16 * 12)
            pe.wait_ge(consts_ready, 2)
            for g in range(RG):
                pe.wait_ge(norm_ready.sem, norm_ready.at(g, 1))
                if g:
                    pe.wait_ge(feat_ready.sem, 4 * g)
                for c in range(NC):
                    for u in range(2):
                        for t in range(4):
                            ins = pe.transpose(turned[2 * c + u][:, t * P:(t + 1) * P],
                                               rows[g % 2][:, 0, 4 * u + t, c * P:(c + 1) * P], eye[:])
                        ins.then_inc(turned_ready.sem, 1)
                pe.wait_ge(feat_ready.sem, 4 * (g + 1))
                for q in range(RQ):
                    for c in range(NC):
                        ins = pe.matmul(logit_bank[:, E * q:E * (q + 1)], feat[:, c, q * P:(q + 1) * P],
                                        router[:, c, :], start=c == 0, stop=c == NC - 1)
                ins.then_inc(logits_ready.sem, 1)
                pe.wait_ge(chosen_ready.sem, chosen_ready.at(g, 1))
                flat = chosen_bf[:].rearrange("p q e -> p (q e)")
                pe.matmul(rank_bank[:, 0:RQ * E], before_bf[:], flat, start=True, stop=False)
                for d in range(1, RQ):
                    pe.matmul(rank_bank[:, E * d:E * RQ], ones_bf[:], flat[:, 0:E * (RQ - d)],
                              start=False, stop=d == RQ - 1)
                for q in range(RQ):
                    ins = pe.matmul(rank_bank[:, RQ * E:(RQ + 1) * E], ones_bf[:], flat[:, E * q:E * (q + 1)],
                                    start=q == 0, stop=q == RQ - 1)
                ins.then_inc(ranks_ready.sem, 1)


def swiglu(nc, weights, eye, where=None, regions=None, shares=None, x2_dram=None, out=None):
    shared = x2_dram is not None
    name = "s_" if shared else "e_"
    up_hi, up_lo, down_hi, down_lo = weights
    units = TOKENS // P if shared else SLOT_TILES
    ctx = ExitStack()
    with ctx:
        def sb(n, shape, dt=F32):
            return ctx.enter_context(nc.sbuf_tensor(name + n, shape, dt))

        def bank(n):
            return ctx.enter_context(nc.psum_tensor(name + n, [P, 512], F32))

        def sem(n):
            return ctx.enter_context(nc.semaphore(name + n))

        rows = [sb(f"rows{n}", [P, ROW]) for n in range(UNROLL)]
        x_hi = [sb(f"x_hi{n}", [P, D], F32R) for n in range(2)]
        x_lo = [sb(f"x_lo{n}", [P, D], F32R) for n in range(2)]
        tanh = [sb(f"tanh{n}", [P, HID]) for n in range(2)]
        gated = [sb(f"gated{n}", [P, HID]) for n in range(2)]
        hidden = [sb(f"hidden{n}", [P, HID]) for n in range(2)]
        hid_hi = [sb(f"hid_hi{n}", [P, HID], F32R) for n in range(2)]
        hid_lo = [sb(f"hid_lo{n}", [P, HID], F32R) for n in range(2)]
        y = [sb(f"y{n}", [P, D]) for n in range(UNROLL)]
        turned_x = [bank(f"turned_x{n}") for n in range(2)]
        ups = [bank(f"ups{n}") for n in range(2)]
        turned = [bank(f"turned{n}") for n in range(2)]
        downs = [bank(f"downs{n}") for n in range(2)]

        loaded = [sem(f"loaded{n}") for n in range(UNROLL)]
        stored = [sem(f"stored{n}") for n in range(UNROLL)]
        turned_x_ready = Flow(sem("turned_x_ready"))
        x_hi_done = Flow(sem("x_hi_done"))
        x_ready = Flow(sem("x_ready"), 2)
        ups_ready = Flow(sem("ups_ready"), 2)
        tanh_done = Flow(sem("tanh_done"))
        gated_ready = Flow(sem("gated_ready"))
        ups_free = Flow(sem("ups_free"), UNROLL)
        turned_ready = Flow(sem("turned_ready"))
        hid_hi_done = Flow(sem("hid_hi_done"))
        hid_ready = Flow(sem("hid_ready"), 2)
        downs_ready = Flow(sem("downs_ready"), 2)
        y_ready = Flow(sem("y_ready"), UNROLL)
        pool_pause, pause = sem("pool_pause"), sem("pause")
        if shared:
            x_norm = [sb(f"x_norm{n}", [P, D]) for n in range(2)]
            share = [[sb(f"share{k}{n}", [P, D]) for n in range(UNROLL)] for k in range(2)]
            total = [sb(f"total{n}", [P, D]) for n in range(UNROLL)]
            stats = [sb(f"stats{n}", [P, 6]) for n in range(2)]
            mean_var = [sb(f"mean_var{n}", [P, 2]) for n in range(2)]
            rstd = [sb(f"rstd{n}", [P, 1]) for n in range(2)]
            power = sb("power", [P, 1])
            share_loaded = [[sem(f"share{k}_loaded{n}") for n in range(UNROLL)] for k in range(2)]
            stats_ready = Flow(sem("stats_ready"))
            var_ready = Flow(sem("var_ready"))
            eps_added = Flow(sem("eps_added"))
            rstd_ready = Flow(sem("rstd_ready"))
            norm_ready = Flow(sem("norm_ready"))
            share_step = Flow(sem("share_step"))
            shares_added = Flow(sem("shares_added"))
        else:
            place = [sb(f"place{n}", [P, 1], U32) for n in range(UNROLL)]
            place_ready = Flow(sem("place_ready"), UNROLL)
            share_step = place_ready

        def times(u, r):
            return 4 * u + (16 - 4 * r)

        assert 16 == 4 * UNROLL

        def wait_stored(engine, u, r):
            if not isinstance(u, int) or u >= UNROLL:
                engine.wait_ge(stored[r], times(u, r) - 16)

        block = ctx.enter_context(nc.Block())

        @block.sync
        def _(sp):
            if shared:
                x2t = x2_dram.rearrange("b t d -> (b t) d")
                outt = out.rearrange("b t d -> (b t) d")

                def load(u, r):
                    if not isinstance(u, int) or u >= UNROLL:
                        sp.wait_ge(norm_ready.sem, norm_ready.at(u, 1 - UNROLL))
                        sp.wait_ge(shares_added.sem, shares_added.at(u, 1 - UNROLL))
                    sp.dma_start(rows[r][:, 0:D], x2t[bass.ds(P * u, P), :]).then_inc(loaded[r], 16)
                    for k in range(2):
                        sp.dma_start(share[k][r][:], shares[bass.ds(P * u + k * TOKENS, P), :])\
                          .then_inc(share_loaded[k][r], 16)

                def store(u, r):
                    sp.wait_ge(y_ready.sem, y_ready.at(u, 1))
                    sp.dma_start(outt[bass.ds(P * u, P), :], y[r][:]).then_inc(stored[r], 16)

                run_pipeline(sp, units, ((0, load), (6, store)))
                for r in range(UNROLL):
                    sp.wait_ge(stored[r], 16 * (units // UNROLL))
            else:
                with sp.Fori(0, units // UNROLL) as i:
                    for r in range(UNROLL):
                        u = UNROLL * i + r
                        sp.wait_ge(ups_free.sem, ups_free.at(u, 1 - UNROLL))
                        sp.wait_ge(place_ready.sem, place_ready.at(u, 1 - UNROLL))
                        row = sp.value_load(where[0:1, 0, bass.ds(u, 1)], min_val=0,
                                            max_val=E * REGION + (PAD_TILES - 1) * P)
                        sp.dma_start(rows[r][:], regions[bass.ds(row, P), :]).then_inc(loaded[r], 16)

        @block.gpsimd
        def _(pool):
            if shared:
                pool.memset(power[:], -0.5)

                def rstd_of(u, r):
                    s = r % 2
                    pool.wait_ge(var_ready.sem, var_ready.at(u, 1))
                    pool.sem_inc(pool_pause, 1)
                    pool.tensor_scalar(rstd[s][:], mean_var[s][:, 1:2], EPS, None, ALU.add)\
                        .then_inc(eps_added.sem, 1)
                    pool.wait_ge(eps_added.sem, eps_added.at(u, 1))
                    pool.tensor_tensor(rstd[s][:], rstd[s][:], power[:], ALU.pow).then_inc(rstd_ready.sem, 1)

                def add_shares(u, r):
                    for k in range(2):
                        pool.wait_ge(share_loaded[k][r], times(u, r))
                    if not isinstance(u, int) or u >= UNROLL:
                        pool.wait_ge(y_ready.sem, y_ready.at(u, 1 - UNROLL))
                    pool.tensor_tensor(total[r][:], share[0][r][:], share[1][r][:], ALU.add)\
                        .then_inc(share_step.sem, 1)
                    pool.wait_ge(share_step.sem, share_step.at(u, 1))
                    pool.tensor_tensor(total[r][:], total[r][:], rows[r][:, 0:D], ALU.add)\
                        .then_inc(shares_added.sem, 1)

                run_pipeline(pool, units, ((0, rstd_of), (1, add_shares)))
            else:
                pool.sem_inc(place_ready.sem, UNROLL)

                def read_place(u, r):
                    pool.wait_ge(loaded[r], times(u, r))
                    wait_stored(pool, u, r)
                    pool.sem_inc(pool_pause, 1)
                    pool.tensor_copy(place[r][:], rows[r][:, D + 1:D + 2]).then_inc(place_ready.sem, 1)

                def scatter(u, r):
                    pool.wait_ge(place_ready.sem, place_ready.at(u, 1))
                    pool.wait_ge(y_ready.sem, y_ready.at(u, 1))
                    pool.sem_inc(pool_pause, 1)
                    pool.indirect_dma_start(shares, bass.IndirectOffsetOnAxis(place[r][:, 0:1], 0),
                                            y[r][:], None).then_inc(stored[r], 16)

                run_pipeline(pool, units, ((0, read_place), (3, scatter)))
                for n in range(UNROLL):
                    pool.wait_ge(stored[n], 16 * (units // UNROLL))

        lag = 1 if shared else 0

        @block.scalar
        def _(act):
            def x_part(u, r):
                s = r % 2
                act.wait_ge(turned_x_ready.sem, turned_x_ready.at(u, 1))
                act.wait_ge(ups_ready.sem, ups_ready.at(u, -1))
                act.copy(x_hi[s][:], turned_x[s][:, 0:D]).then_inc(x_hi_done.sem, 1)

            def tanh_part(u, r):
                s = r % 2
                act.wait_ge(ups_ready.sem, ups_ready.at(u, 1))
                act.activation(tanh[s][:], ups[s][:, 0:HID], ACT.Tanh, scale=0.5).then_inc(tanh_done.sem, 1)

            def hidden_part(u, r):
                s = r % 2
                act.wait_ge(turned_ready.sem, turned_ready.at(u, 1))
                act.wait_ge(downs_ready.sem, downs_ready.at(u, -1))
                act.copy(hid_hi[s][:], turned[s][:, 0:HID]).then_inc(hid_hi_done.sem, 1)

            def output(u, r):
                act.wait_ge(downs_ready.sem, downs_ready.at(u, 1))
                wait_stored(act, u, r)
                act.copy(y[r][:], downs[r % 2][:, 0:D]).then_inc(y_ready.sem, 1)

            stages = ((lag, x_part), (lag + 1, tanh_part), (lag + 2, hidden_part))
            run_pipeline(act, units, stages if shared else stages + ((lag + 3, output),))

        @block.vector
        def _(dve):
            dve.sem_inc(x_ready.sem, 2)
            dve.sem_inc(ups_free.sem, UNROLL)
            dve.sem_inc(hid_ready.sem, 2)
            dve.sem_inc(y_ready.sem, UNROLL)

            def normalise(u, r):
                s = r % 2
                dve.wait_ge(loaded[r], times(u, r))
                dve.bn_stats(stats[s][:], rows[r][:, 0:D]).then_inc(stats_ready.sem, 1)
                dve.wait_ge(stats_ready.sem, stats_ready.at(u, 1))
                dve.sem_inc(pause, 1)
                dve.bn_aggr(mean_var[s][:], stats[s][:]).then_inc(var_ready.sem, 1)

            def scale(u, r):
                s = r % 2
                dve.wait_ge(rstd_ready.sem, rstd_ready.at(u, 1))
                dve.tensor_scalar(x_norm[s][:], rows[r][:, 0:D], mean_var[s][:, 0:1], rstd[s][:, 0:1],
                                  ALU.subtract, ALU.mult).then_inc(norm_ready.sem, 1)

            def x_part(u, r):
                s = r % 2
                dve.wait_ge(x_hi_done.sem, x_hi_done.at(u, 1))
                dve.tensor_tensor(x_lo[s][:], turned_x[s][:, 0:D], x_hi[s][:].bitcast(F32),
                                  ALU.subtract).then_inc(x_ready.sem, 1)

            def gate(u, r):
                s = r % 2
                dve.wait_ge(tanh_done.sem, tanh_done.at(u, 1))
                dve.scalar_tensor_tensor(out=gated[s][:], in0=tanh[s][:], scalar=1.0, in1=ups[s][:, 0:HID],
                                         op0=ALU.add, op1=ALU.mult).then_inc(gated_ready.sem, 1)
                dve.wait_ge(gated_ready.sem, gated_ready.at(u, 1))
                dve.scalar_tensor_tensor(out=hidden[s][:], in0=gated[s][:],
                                         scalar=0.5 if shared else rows[r][:, D:D + 1],
                                         in1=ups[s][:, HID:2 * HID], op0=ALU.mult, op1=ALU.mult)\
                    .then_inc(ups_free.sem, 1)

            def hidden_part(u, r):
                s = r % 2
                dve.wait_ge(hid_hi_done.sem, hid_hi_done.at(u, 1))
                dve.tensor_tensor(hid_lo[s][:], turned[s][:, 0:HID], hid_hi[s][:].bitcast(F32),
                                  ALU.subtract).then_inc(hid_ready.sem, 1)

            def output(u, r):
                dve.wait_ge(downs_ready.sem, downs_ready.at(u, 1))
                dve.wait_ge(shares_added.sem, shares_added.at(u, 1))
                wait_stored(dve, u, r)
                dve.tensor_tensor(y[r][:], downs[r % 2][:, 0:D], total[r][:], ALU.add)\
                    .then_inc(y_ready.sem, 1)

            stages = ((lag, x_part), (lag + 1, gate), (lag + 2, hidden_part))
            if shared:
                stages = ((1, scale), (0, normalise)) + stages + ((lag + 3, output),)
            run_pipeline(dve, units, stages)

        @block.tensor
        def _(pe):
            pe.sem_inc(ups_ready.sem, 2)
            pe.sem_inc(downs_ready.sem, 2)

            def passes(bank_part, pairs):
                todo = [(w, x) for (wh, wl), (xh, xl) in pairs for w, x in ((wh, xh), (wl, xh), (wh, xl))]
                for j, (w, x) in enumerate(todo):
                    ins = pe.matmul(bank_part, w, x, start=j == 0, stop=j == len(todo) - 1)
                return ins

            def expert(u):
                if shared:
                    return slice(E, E + 1)
                return bass.ds(pe.value_load(where[0:1, 1, bass.ds(u, 1)], min_val=0, max_val=E - 1), 1)

            def of(w, e, c):
                return w[:, e, c, :].rearrange("p o n -> p (o n)")

            def turn_x(u, r):
                s = r % 2
                if shared:
                    pe.wait_ge(norm_ready.sem, norm_ready.at(u, 1))
                else:
                    pe.wait_ge(loaded[r], times(u, r))
                pe.wait_ge(x_ready.sem, x_ready.at(u, -1))
                src = x_norm[s] if shared else rows[r]
                for c in range(NC):
                    ins = pe.transpose(turned_x[s][:, c * P:(c + 1) * P], src[:, c * P:(c + 1) * P], eye[:])
                ins.then_inc(turned_x_ready.sem, 1)

            def up(u, r):
                s = r % 2
                e = expert(u)
                pe.wait_ge(x_ready.sem, x_ready.at(u, 1))
                pe.wait_ge(ups_free.sem, ups_free.at(u, -1))
                passes(ups[s][:], [((x_hi[s][:, c * P:(c + 1) * P], x_lo[s][:, c * P:(c + 1) * P]),
                                    (of(up_hi, e, c), of(up_lo, e, c))) for c in range(NC)])\
                    .then_inc(ups_ready.sem, 1)

            def turn_hidden(u, r):
                s = r % 2
                pe.wait_ge(ups_free.sem, ups_free.at(u, 1))
                pe.wait_ge(hid_ready.sem, hid_ready.at(u, -1))
                for c in range(HID // P):
                    ins = pe.transpose(turned[s][:, c * P:(c + 1) * P], hidden[s][:, c * P:(c + 1) * P], eye[:])
                ins.then_inc(turned_ready.sem, 1)

            def down(u, r):
                s = r % 2
                e = expert(u)
                pe.wait_ge(hid_ready.sem, hid_ready.at(u, 1))
                pe.wait_ge(y_ready.sem, y_ready.at(u, -1))
                passes(downs[s][:, 0:D], [((hid_hi[s][:, c * P:(c + 1) * P], hid_lo[s][:, c * P:(c + 1) * P]),
                                           (of(down_hi, e, c), of(down_lo, e, c))) for c in range(HID // P)])\
                    .then_inc(downs_ready.sem, 1)

            run_pipeline(pe, units, ((lag, turn_x), (lag + 1, up), (lag + 2, turn_hidden), (lag + 3, down)))


def constants():
    start = 2.0 ** (-2.0 ** (-(np.log2(H) - 3)))
    slopes = np.array([start * start ** i for i in range(H)], np.float32)
    bias = -(slopes[:, None] * np.arange(T, dtype=np.float32)[None, :]).astype(np.float32)
    hi = (bias.view(np.uint32) & np.uint32(0xFFFFF000)).view(np.float32)
    alibi = np.stack([hi, bias - hi]).reshape(2, H // 2, NQ, D)
    k = np.arange(P)
    tri = np.where(k[:, None] > k[None, :], MASKED, 0.0).astype(np.float32)
    row_mask = np.zeros((P, T), np.float32)
    row_mask[:, T - P:] = tri.T
    head_mask = np.repeat((k[:, None] // DH == np.arange(HC)[None, :])[:, :, None], M, 2)
    pick = np.zeros((2 * 32, H // 2, P), np.float32)
    for h in range(H):
        for r in (h, 32 + h):
            pick[r, h // 2, M * (h % 2):M * (h % 2 + 1)] = 1.0
    return {"eye": np.eye(P, dtype=np.float32), "tri": tri, "row_mask": row_mask,
            "head_mask": head_mask.astype(np.float32), "pick_max": pick.reshape(2 * 32, NQ, D),
            "alibi": alibi, **routing_tables()}


def routing_tables():
    p = np.arange(P)
    rows = {"expert_no": np.arange(E), "region_start": np.arange(E + 1) * REGION,
            "up_to": (np.arange(E)[None, :] <= np.arange(E)[:, None]).astype(int),
            "tile_no": np.arange(SLOT_TILES), "tile_start": np.arange(TOKENS // P) * P}
    tables = {n: np.broadcast_to(v, (P,) + v.shape) for n, v in rows.items()}
    k, q = np.arange(2)[None, :, None], np.arange(RQ)[None, None, :]
    tables["dest"] = k * TOKENS + q * P + p[:, None, None]
    tables["pad_dest"] = PAIRS + (k * RQ + q) * P + p[:, None, None]
    tables["part_no"] = p[:, None]
    tables["before"] = p[:, None] < p[None, :]
    return {n: v.astype(np.float32) for n, v in tables.items()}


def layouts(v):
    kv = v["L0_xattn_Wkv"].reshape(H, 2, DH, DC)
    bkv = v["L0_xattn_bkv"].reshape(H, 2, DH)
    ups = [np.concatenate([w1, w3], -1) for w1, w3 in zip(v["L0_ffn_w1"], v["L0_ffn_w3"])]
    ups.append(np.concatenate([v["L0_ffn_sw1"], v["L0_ffn_sw3"]], -1))
    d = {"x": v["x"], "ctx": v["ctx_768"].transpose(0, 2, 1),
         "w_xk": kv[:, 0].reshape(D, DC).T, "w_xv": kv[:, 1].reshape(D, DC).T,
         "w_xq": v["L0_xattn_Wq"].T, "w_xo": v["L0_xattn_Wo"].T, "w_p": v["L0_attn_Wp"].T,
         "xq_bias": v["L0_xattn_bq"].reshape(NC, P).T, "xk_bias": bkv[:, 0].reshape(NC, P).T,
         "xv_bias": np.broadcast_to(bkv[:, 1].reshape(1, D), (P, D)),
         "xo_bias": np.broadcast_to(v["L0_xattn_bo"], (P, D)),
         "w_up": np.stack(ups),
         "w_down": np.concatenate([v["L0_ffn_w2"], v["L0_ffn_sw2"][None]], 0),
         "router_w": v["L0_ffn_router_w"],
         "expert_bias": np.broadcast_to(v["L0_ffn_expert_bias"], (P, E))}
    for n in "qkv":
        d["w_" + n] = v["L0_attn_W" + n].T
        d["a_" + n] = v["L0_attn_A" + n].T
        d["b_" + n] = v["L0_attn_B" + n]
    return d


def kernel(**inputs):
    import concourse.bacc as bacc
    from concourse.bass_utils import run_bass_kernel_spmd

    nc = bacc.Bacc("TRN2", target_bir_lowering=False, num_devices=1)
    arrays, aps = {}, {}
    host = {**layouts({k: np.asarray(v) for k, v in inputs.items()}), **constants()}
    for name, value in host.items():
        arrays["in_" + name] = np.ascontiguousarray(value)
        aps[name] = nc.dram_tensor("in_" + name, value.shape, F32, kind="ExternalInput").ap()
    out = nc.dram_tensor("out", (B, T, D), F32, kind="ExternalOutput").ap()
    x2 = nc.dram_tensor("x2", (B, T, D), F32, kind="Internal").ap()
    attention(nc, aps, x2)
    mixture(nc, aps, x2, out)
    r = run_bass_kernel_spmd(nc, [arrays], core_ids=[0])
    return r.results[0]["out"]
```
